# Optimizing a Trainium2 kernel written in Bass

```python
import numpy as np
import jax
import jax.numpy as jnp

def _softmax(x, axis=-1):
    return jax.nn.softmax(x, axis=axis)

def _gelu(x):
    return jax.nn.gelu(x, approximate=True)

def _silu(x):
    return jax.nn.silu(x)

def _sigmoid(x):
    return jax.nn.sigmoid(x)

def _layernorm(x, axis=-1, eps=1e-05):
    m = jnp.mean(x, axis=axis, keepdims=True)
    v = jnp.var(x, axis=axis, keepdims=True)
    return (x - m) / jnp.sqrt(v + eps)

def _scatter_add(tgt, idx, src, axis=0):
    return tgt.at[idx].add(src)

def _segment_sum(src, seg, n):
    return jax.ops.segment_sum(src, seg, n)
kernel_name = 'mk_gnn_resnorm_d1_gnn_r8_a44dc2'

def setup_inputs(seed: int=0):
    np.random.seed(seed)
    _w = jnp.asarray

    def _rec_inputs():
        import jax
        import jax.numpy as jnp
        _gk = jax.random.key(seed)
        x = -6.415e-05 + 1 * jax.random.normal(jax.random.fold_in(_gk, 1), (1250, 512), jnp.float32)
        src = jax.random.randint(jax.random.fold_in(_gk, 2), (40000,), 0, 1250, jnp.int32)
        dst = jax.random.randint(jax.random.fold_in(_gk, 3), (40000,), 0, 1250, jnp.int32)
        _o = jnp.argsort(dst, stable=True)
        src = src[_o]
        dst = dst[_o]
        edge_type_32 = jax.random.randint(jax.random.fold_in(_gk, 12), (40000,), 0, 32, jnp.int32)
        edge_weight1 = jax.random.uniform(jax.random.fold_in(_gk, 13), (40000, 1), jnp.float32, 0.0, 0.999996)
        return (x, src, dst, edge_type_32, edge_weight1)
    x, src, dst, edge_type_32, edge_weight1 = _rec_inputs()

    def _L0_gnn_setup():
        import jax, jax.numpy as jnp
        import numpy as np
        N_NODES = 2500
        N_EDGES = 40000
        IN_FEAT = 512
        OUT_FEAT = 512
        NUM_RELS = 32
        NUM_BASES = 8
        key = jax.random.key(seed)
        ks = jax.random.split(key, 8)
        x = jax.random.normal(ks[0], (N_NODES, IN_FEAT), dtype=jnp.float32)
        bases = jax.random.normal(ks[1], (NUM_BASES, IN_FEAT, OUT_FEAT), dtype=jnp.float32) * (1.0 / np.sqrt(IN_FEAT))
        w_comp = jax.random.normal(ks[2], (NUM_RELS, NUM_BASES), dtype=jnp.float32) * (1.0 / np.sqrt(NUM_BASES))
        h_bias = jnp.zeros((OUT_FEAT,), dtype=jnp.float32)
        norm = jax.random.uniform(ks[3], (N_EDGES, 1), dtype=jnp.float32)
        src = jax.random.randint(ks[4], (N_EDGES,), 0, N_NODES, dtype=jnp.int32)
        dst = jax.random.randint(ks[5], (N_EDGES,), 0, N_NODES, dtype=jnp.int32)
        etype = jnp.sort(jax.random.randint(ks[6], (N_EDGES,), 0, NUM_RELS, dtype=jnp.int32))
        return {'x': x, 'bases': bases, 'w_comp': w_comp, 'h_bias': h_bias, 'norm': norm, 'src': src, 'dst': dst, 'etype': etype}
    _L0_gnn_all = _L0_gnn_setup()
    _L0_gnn_in = {k: v for k, v in _L0_gnn_all.items() if k in ('bases', 'w_comp', 'h_bias')}
    del _L0_gnn_all
    return {'x': x, 'src': src, 'dst': dst, 'edge_type_32': edge_type_32, 'edge_weight1': edge_weight1, 'L0_gnn_bases': _L0_gnn_in['bases'], 'L0_gnn_w_comp': _L0_gnn_in['w_comp'], 'L0_gnn_h_bias': _L0_gnn_in['h_bias']}

def reference(x, src, dst, edge_type_32, edge_weight1, L0_gnn_bases, L0_gnn_w_comp, L0_gnn_h_bias):
    import jax
    import jax.numpy as jnp

    def _L0_gnn_ref(x, bases, w_comp, h_bias, norm, src, dst, etype):
        import jax, jax.numpy as jnp
        import numpy as np
        N_NODES = 2500
        N_EDGES = 40000
        IN_FEAT = 512
        OUT_FEAT = 512
        NUM_RELS = 32
        NUM_BASES = 8
        n_nodes = x.shape[0]
        weight = jnp.einsum('rb,bio->rio', w_comp, bases)
        h_rel = jnp.einsum('ni,rio->rno', x, weight)
        msg = h_rel[etype, src] * norm
        out = jax.ops.segment_sum(msg, dst, num_segments=n_nodes)
        out = out + h_bias
        return out
    x = _layernorm(x + _L0_gnn_ref(x, L0_gnn_bases, L0_gnn_w_comp, L0_gnn_h_bias, edge_weight1, src, dst, edge_type_32), axis=-1)
    return x

_drawn_inputs = setup_inputs


def setup_inputs(seed=0):
    import zlib

    import numpy as np

    out = dict(_drawn_inputs(seed))
    spreads = {'L0_gnn_h_bias': (0.0, 0.277)}
    factors = {}
    for name, (base, spread) in spreads.items():
        noise = np.random.default_rng([zlib.crc32(name.encode()), seed]).standard_normal(out[name].shape)
        drawn = base * np.exp(spread * noise) if base else spread * noise
        out[name] = jnp.asarray(drawn.astype(out[name].dtype))
    for name, factor in factors.items():
        out[name] = (out[name] * factor).astype(out[name].dtype)
    return out
```

```python
from contextlib import ExitStack

import concourse.bass as bass
from concourse import mybir

ALU = mybir.AluOpType
ACT = mybir.ActivationFunctionType
AX_X = mybir.AxisListType.X
F32 = mybir.dt.float32
I32 = mybir.dt.int32
U32 = mybir.dt.uint32

P = 128
EPS = 1e-5
WIN = 8
BLK = P
RING_BLOCKS = 3
SLOTS = 8
LATE = 8
EARLY = 16
MASKS = 4
PARTS = 4
AHEAD = 2
UNIT = 4
GEN_NODES = 50


def rgcn_resnorm(nc, x, src, dst, etype, weight, bases, w_comp, h_bias, out):
    N, F = x.shape
    E = src.shape[0]
    R, NB = w_comp.shape
    T = -(-E // P)
    LAST = E - (T - 1) * P
    TC = -(-T // P)
    IC = F // P
    PL = IC * NB
    NBLK = -(-N // BLK)
    TPB = E * BLK // (N * P)
    NPT = BLK // TPB
    RING = RING_BLOCKS * BLK
    UNITS = PL // UNIT
    HEAD = TPB + LATE
    GPB = TPB // SLOTS
    NG = -(-T // SLOTS)
    TAIL = HEAD + (NBLK - 2) * TPB
    Q = 4
    QB = 16
    QN = -(-T // Q)
    NQB = -(-QN // QB)
    assert P // R == Q and E * BLK == TPB * N * P and LAST * 2 == P and NG % 2 == 0
    assert HEAD % SLOTS == 0 and PL == TPB and T - (NG - 1) * SLOTS == 1 and N % GEN_NODES == 0

    with ExitStack() as ctx:
        def sb(name, shape, dt=F32):
            return ctx.enter_context(nc.sbuf_tensor(name, shape, dt))

        def psum(name, shape):
            return ctx.enter_context(nc.psum_tensor(name, shape, F32))

        def sem(name):
            return ctx.enter_context(nc.semaphore(name))

        ident = sb("ident", [P, P])
        ones = sb("ones", [P, 1])
        zero = sb("zero", [P, 1])
        eps = sb("eps", [P, 1])
        node_iota = sb("node_iota", [P, GEN_NODES])
        part_no = sb("part_no", [P, 1])
        rel_of_part = sb("rel_of_part", [P, Q])
        tile_nodes = sb("tile_nodes", [P, TC])
        w_diag = sb("w_diag", [P, Q * NB])
        bias_all = sb("bias_all", [P, F])
        src_i = sb("src_i", [P, TC, P], I32)
        dst_i = sb("dst_i", [P, TC, P], I32)
        src_f = sb("src_f", [P, TC, P])
        dst_f = sb("dst_f", [P, TC, P])
        rel_f = sb("rel_f", [P, TC, P])
        wgt_t = sb("wgt_t", [P, TC, P])
        base = sb("base", [P, TC])
        top = sb("top", [P, TC])
        chk = sb("chk", [P, 4, TC])
        bad = sb("bad", [P, 1])
        pos = sb("pos", [P, 4, TC])
        pos_row = sb("pos_row", [1, TC * P], I32)
        flag = sb("flag", [1, 1], I32)
        idx = sb("idx", [P, TC * P], U32)
        rel = sb("rel", [P, TC * P])
        dstc = sb("dstc", [P, TC * P])
        wgt = sb("wgt", [P, TC * P])
        coef = sb("coef", [P, QB * NQB * Q, NB])
        et_i = sb("et_i", [P, 2, QB, P], I32)
        et_hot = sb("et_hot", [P, 2, QB, P])
        bases_sb = sb("bases_sb", [P, IC, NB, F])
        rows = sb("rows", [P, SLOTS, F])
        idx_s = sb("idx_s", [P, 2, SLOTS], U32)
        win = sb("win", [P, MASKS, NB, WIN])
        sums = sb("sums", [P, PL, RING + WIN])
        unit = sb("unit", [P, 2, UNIT, BLK])
        xres = sb("xres", [P, F])
        y = sb("y", [P, F])
        stats = sb("stats", [P, 6])
        mv = sb("mv", [P, 2])
        sd = sb("sd", [P, 4])
        gidx = sb("gidx", [P, 1], U32)
        gwin = sb("gwin", [P, NB, GEN_NODES])
        gsum = sb("gsum", [P, IC, NB, GEN_NODES])
        banks = psum("banks", [P, 8, 512])
        part = banks[:, 0:PARTS, 0:PL * WIN]
        out_ps = banks[:, 6, :]
        small_ps = banks[:, 7, :]

        src_in, dst_in, wgt_in = sem("src_in"), sem("dst_in"), sem("wgt_in")
        const_in = sem("const_in")
        et_in = [sem("et_in0"), sem("et_in1")]
        bases_in = [sem(f"bases_in{c}") for c in range(IC)]
        consts, pool_c = sem("consts"), sem("pool_c")
        cleared, prep, chained = sem("cleared"), sem("prep"), sem("chained")
        transposed, tables = sem("transposed"), sem("tables")
        hot_ready, coef_ps, coef_ready = sem("hot_ready"), sem("coef_ps"), sem("coef_ready")
        row_in = [sem(f"row_in{s}") for s in range(SLOTS)]
        idx_in = [sem("idx_in0"), sem("idx_in1")]
        flag_ready = sem("flag_ready")
        turns, dve_turns, act_turns = sem("turns"), sem("dve_turns"), sem("act_turns")
        win_ready, part_ready, part_added = sem("win_ready"), sem("part_ready"), sem("part_added")
        folded, unit_ready, unit_free = sem("folded"), sem("unit_ready"), sem("unit_free")
        cleaned = sem("cleaned")
        block_done, evacuated = sem("block_done"), sem("evacuated")
        x_in, out_written = sem("x_in"), sem("out_written")
        norm_v, norm_a = sem("norm_v"), sem("norm_a")
        g_step, g_idx, g_row, g_win, g_mm = sem("g_step"), sem("g_idx"), sem("g_row"), sem("g_win"), sem("g_mm")
        g_sum, g_out, g_v, g_a, g_x, g_w = sem("g_sum"), sem("g_out"), sem("g_v"), sem("g_a"), sem("g_x"), sem("g_w")

        TL = T - (TC - 1) * P
        full = (TC - 1) * P * P

        def tile_major(a):
            flat = a.rearrange("e o -> (e o)") if len(a.shape) == 2 else a
            return (flat[0:full].rearrange("(c p e) -> p c e", p=P, e=P),
                    flat[full:full + (TL - 1) * P].rearrange("(p e) -> p e", e=P),
                    flat[E - LAST:E].unsqueeze(0))

        def block_rows(k):
            return slice(k * BLK, min(N, (k + 1) * BLK))

        with nc.Block() as block:

            @block.sync
            def _(sp):
                for n, (a, t, s) in enumerate(((src, src_i, src_in), (dst, dst_i, dst_in), (weight, wgt_t, wgt_in))):
                    body, rest, half = tile_major(a)
                    sp.dma_start(t[:, 0:TC - 1, :], body).then_inc(s, 16)
                    sp.wait_ge(cleared, n + 1)
                    sp.dma_start(t[0:TL - 1, TC - 1, :], rest).then_inc(s, 16)
                    sp.dma_start(t[TL - 1:TL, TC - 1, 0:LAST], half).then_inc(s, 16)
                    if a is not weight:
                        sp.dma_start(t[TL - 1:TL, TC - 1, LAST:P], half).then_inc(s, 16)
                sp.wait_ge(cleared, 4)
                for j in range(Q):
                    sp.dma_start(w_diag[R * j:R * j + R, NB * j:NB * j + NB], w_comp).then_inc(const_in, 16)
                sp.dma_start(bias_all[:, :], h_bias.partition_broadcast(P)).then_inc(const_in, 16)
                for n in range(NQB):
                    if n >= 2:
                        sp.wait_ge(hot_ready, n - 1)
                    if n == NQB - 1:
                        sp.wait_ge(cleared, 5)
                    for j in range(Q):
                        nq = min(QB, (T - 1) // Q - n * QB)
                        a = etype[n * QB * Q * P:(n * QB + nq) * Q * P].rearrange("(q j e) -> j q e", j=Q, e=P)
                        sp.dma_start(et_i[R * j:R * j + R, n % 2, 0:nq, :], a[j].partition_broadcast(R)).then_inc(et_in[n % 2], 16)
                    if n == NQB - 1:
                        sp.dma_start(et_i[0:R, n % 2, nq, 0:LAST], etype[E - LAST:E].partition_broadcast(R)).then_inc(et_in[n % 2], 16)
                for c in range(IC):
                    sp.dma_start(bases_sb[:, c, :, :], bases[:, c * P:(c + 1) * P, :].rearrange("b p o -> p b o")).then_inc(bases_in[c], 16)
                sp.wait_ge(flag_ready, 1)
                ok = sp.value_load(flag[0:1, 0:1], min_val=0, max_val=1)
                with sp.If(ok == 1):
                    def stage(g, par, wait):
                        if wait is not None:
                            sp.wait_ge(row_in[SLOTS - 1], wait)
                        sp.dma_start(idx_s[:, par, :], idx[:, bass.ds(g * SLOTS, SLOTS)]).then_inc(idx_in[par], 16)
                    stage(1, 1, None)
                    with sp.Fori(1, NG // 2) as h:
                        stage(2 * h, 0, 32 * h - 16)
                        stage(2 * h + 1, 1, 32 * h)
                with sp.Else():
                    sp.nop()

            @block.gpsimd
            def _(pool):
                nc.gpsimd.memset(ident[:, :], 0.0).then_inc(pool_c, 1)
                pool.wait_ge(pool_c, 1)
                nc.gpsimd.affine_select(out=ident[:, :], in_=ident[:, :], compare_op=ALU.not_equal, fill=1.0,
                                        base=0, pattern=[[-1, P]], channel_multiplier=1).then_inc(consts, 1)
                nc.gpsimd.iota(node_iota[:, :], [[1, GEN_NODES]], base=0, channel_multiplier=0,
                               allow_small_or_imprecise_dtypes=True).then_inc(consts, 1)
                nc.gpsimd.iota(tile_nodes[:, :], [[NPT * P, TC]], base=0, channel_multiplier=NPT,
                               allow_small_or_imprecise_dtypes=True).then_inc(consts, 1)
                nc.gpsimd.iota(part_no[:, :], [[1, 1]], base=0, channel_multiplier=1,
                               allow_small_or_imprecise_dtypes=True).then_inc(consts, 1)

                def gather(s, index, where=rows):
                    return pool.indirect_dma_start(where[:, s, :], None, x, bass.IndirectOffsetOnAxis(index, 0))

                pool.wait_ge(tables, 1)
                for s in range(SLOTS):
                    gather(s, idx[:, s:s + 1]).then_inc(row_in[s], 16)
                pool.wait_ge(flag_ready, 1)
                ok = pool.value_load(flag[0:1, 0:1], min_val=0, max_val=1)
                with pool.If(ok == 1):
                    def group(par, idx_wait, first_tile, slots=SLOTS):
                        pool.wait_ge(idx_in[par], idx_wait)
                        pool.sem_inc(turns, 1)
                        for s in range(slots):
                            pool.wait_ge(part_ready, first_tile + s - SLOTS + 1)
                            pool.sem_inc(turns, 1)
                            gather(s, idx_s[:, par, s:s + 1]).then_inc(row_in[s], 16)
                    group(1, 16, SLOTS)
                    with pool.Fori(1, NG // 2 - 1) as h:
                        group(0, 16 * h, 2 * SLOTS * h)
                        group(1, 16 * h + 16, 2 * SLOTS * h + SLOTS)
                    h = NG // 2 - 1
                    group(0, 16 * h, 2 * SLOTS * h)
                    group(1, 16 * h + 16, 2 * SLOTS * h + SLOTS, 1)
                with pool.Else():
                    for s in range(SLOTS):
                        pool.wait_ge(row_in[s], 16)
                    with pool.Fori(0, T * (N // GEN_NODES)) as i:
                        pool.wait_ge(g_idx, i + 1)
                        pool.sem_inc(turns, 1)
                        gather(0, gidx[:, 0:1]).then_inc(g_row, 16)

            @block.tensor
            def _(pe):
                pe.wait_ge(consts, 1)
                for n, (a, s, v) in enumerate(((src_f, prep, 1), (rel_f, prep, 2), (wgt_t, wgt_in, 48), (dst_f, prep, 3))):
                    pe.wait_ge(s, v)
                    for c in range(TC):
                        m = nc.tensor.transpose(banks[:, n, c * P:(c + 1) * P], a[:, c, :], ident[:, :])
                    m.then_inc(transposed, 1)
                pe.wait_ge(prep, 4)
                for c in range(TC):
                    nc.tensor.transpose(small_ps[0:1, c * P:(c + 1) * P], pos[:, 3, c:c + 1], ident[:, :])
                nc.tensor.matmul(out_ps[0:1, 0:1], bad[:, 0:1], ones[:, 0:1], start=True, stop=True).then_inc(transposed, 1)
                pe.wait_ge(const_in, 16 * (Q + 1))
                for n in range(NQB):
                    pe.wait_ge(hot_ready, n + 1)
                    if n >= 2:
                        pe.wait_ge(coef_ready, n - 1)
                    for q in range(min(QB, QN - n * QB)):
                        m = nc.tensor.matmul(banks[:, 4 + n % 2, q * Q * NB:(q + 1) * Q * NB], et_hot[:, n % 2, q, :],
                                             w_diag[:, :], start=True, stop=True)
                    m.then_inc(coef_ps, 1)
                pe.wait_ge(tables, 5)
                pe.wait_ge(flag_ready, 1)
                ok = pe.value_load(flag[0:1, 0:1], min_val=0, max_val=1)
                with pe.If(ok == 1):
                    def tile_product(t, s, row_wait):
                        pe.wait_ge(row_in[s], row_wait)
                        pe.wait_ge(win_ready, t + 1)
                        if not isinstance(t, int) or t >= PARTS:
                            pe.wait_ge(part_added, t - PARTS + 1)
                        for c in range(IC):
                            m = nc.tensor.matmul(part[:, s % PARTS, c * NB * WIN:(c + 1) * NB * WIN],
                                                 rows[:, s, c * P:(c + 1) * P], win[:, s % MASKS, :, :],
                                                 start=True, stop=True)
                        m.then_inc(part_ready, 1)

                    def plane_product(k, p):
                        u = p // UNIT
                        if p % UNIT == 0:
                            pe.wait_ge(unit_ready, k * UNITS + u + 1)
                        if p == 0:
                            pe.wait_ge(evacuated, k + 1)
                        m = nc.tensor.matmul(out_ps, unit[:, u % 2, p % UNIT, :],
                                             bases_sb[:, p // NB, p % NB, :], start=(p == 0), stop=(p == PL - 1))
                        if p % UNIT == UNIT - 1:
                            m.then_inc(unit_free, 1)
                        return m

                    for s in range(SLOTS):
                        tile_product(s, s, 16)
                    with pe.Fori(1, HEAD // SLOTS) as g:
                        for s in range(SLOTS):
                            tile_product(g * SLOTS + s, s, g * 16 + 16)
                    for c in range(IC):
                        pe.wait_ge(bases_in[c], 16)
                    with pe.Fori(0, NBLK - 2) as k:
                        for p in range(PL):
                            tile_product(k * TPB + (HEAD + p), p % SLOTS, k * (GPB * 16) + (HEAD + p) // SLOTS * 16 + 16)
                            m = plane_product(k, p)
                        pe.drain().then_inc(block_done, 1)
                    for p in range(PL):
                        if TAIL + p < T:
                            tile_product(TAIL + p, p % SLOTS, (TAIL + p) // SLOTS * 16 + 16)
                        plane_product(NBLK - 2, p)
                    pe.drain().then_inc(block_done, 1)
                    for p in range(PL):
                        plane_product(NBLK - 1, p)
                    pe.drain().then_inc(block_done, 1)
                with pe.Else():
                    for c in range(IC):
                        pe.wait_ge(bases_in[c], 16)
                    with pe.Fori(0, N // GEN_NODES) as w:
                        def product(i, first):
                            pe.wait_ge(g_row, 16 * i + 16)
                            pe.wait_ge(g_win, i + 1)
                            for c in range(IC):
                                nc.tensor.matmul(banks[:, c, 0:NB * GEN_NODES], rows[:, 0, c * P:(c + 1) * P],
                                                 gwin[:, :, :], start=first, stop=False, skip_group_check=True)
                            pe.drain().then_inc(g_mm, 1)
                        pe.wait_ge(g_sum, w + 1)
                        product(w * T, True)
                        with pe.Fori(1, T) as t:
                            product(w * T + t, False)
                        pe.wait_ge(g_sum, w + 2)
                        pe.wait_ge(g_out, w + 1)
                        for p in range(PL):
                            nc.tensor.matmul(out_ps[0:GEN_NODES, :], gsum[:, p // NB, p % NB, :],
                                             bases_sb[:, p // NB, p % NB, :], start=(p == 0), stop=(p == PL - 1))
                        pe.drain().then_inc(block_done, 1)

            @block.vector
            def _(dve):
                v = nc.vector
                v.memset(src_i[:, TC - 1, :], 0).then_inc(cleared, 1)
                v.memset(dst_i[:, TC - 1, :], 0).then_inc(cleared, 1)
                v.memset(wgt_t[:, TC - 1, :], 0.0).then_inc(cleared, 1)
                v.memset(w_diag[:, :], 0.0).then_inc(cleared, 1)
                v.memset(ones[:, :], 1.0)
                v.memset(zero[:, :], 0.0)
                v.memset(eps[:, :], EPS)
                v.memset(bad[:, :], 0.0)
                dve.wait_ge(src_in, 64)
                v.tensor_copy(src_f[:, :, :], src_i[:, :, :]).then_inc(prep, 1)
                dve.wait_ge(transposed, 1)
                v.tensor_copy(idx[:, :], banks[:, 0, 0:TC * P]).then_inc(tables, 1)
                n_chain = [0]

                def chain(ins):
                    n_chain[0] += 1
                    ins.then_inc(chained, 1)
                    dve.wait_ge(chained, n_chain[0])
                dve.wait_ge(dst_in, 64)
                chain(v.tensor_copy(dst_f[:, :, :], dst_i[:, :, :]))
                v.tensor_reduce(base[:, :], dst_f[:, :, :], AX_X, ALU.min)
                chain(v.tensor_reduce(top[:, :], dst_f[:, :, :], AX_X, ALU.max))
                for c in range(TC):
                    r = v.tensor_scalar(rel_f[:, c, :], dst_f[:, c, :], base[:, c:c + 1], None, ALU.subtract)
                r.then_inc(prep, 2)
                v.tensor_tensor(chk[:, 0, :], top[:, :], base[:, :], ALU.subtract)
                dve.wait_ge(consts, 3)
                v.tensor_tensor(chk[:, 1, :], tile_nodes[:, :], base[:, :], ALU.subtract)
                chain(v.tensor_tensor(chk[:, 2, :], top[:, :], tile_nodes[:, :], ALU.subtract))
                v.tensor_scalar(chk[:, 0, :], chk[:, 0, :], float(WIN), None, ALU.is_ge)
                v.tensor_scalar(chk[:, 1, :], chk[:, 1, :], float(NPT * LATE), None, ALU.is_gt)
                chain(v.tensor_scalar(chk[:, 2, :], chk[:, 2, :], float(NPT * EARLY), None, ALU.is_gt))
                chain(v.tensor_tensor(chk[:, 0, :], chk[:, 0, :], chk[:, 1, :], ALU.add))
                chain(v.tensor_tensor(chk[:, 3, :], chk[:, 0, :], chk[:, 2, :], ALU.add))
                chain(v.memset(chk[64:P, 3, TC - 1:TC], 0.0) if TL <= 64 else v.memset(chk[96:P, 3, TC - 1:TC], 0.0))
                chain(v.tensor_reduce(chk[:, 0, 0:1], chk[:, 3, 0:TC - 1], AX_X, ALU.add))
                chain(v.tensor_copy(bad[:, :], chk[:, 0, 0:1]))
                chain(v.tensor_tensor(bad[0:TL, :], chk[0:TL, 0, 0:1], chk[0:TL, 3, TC - 1:TC], ALU.add))
                for m in range(1, -(-N // RING)):
                    chain(v.tensor_scalar(pos[:, m - 1, :], base[:, :], float(m * RING), float(-RING), ALU.is_ge, ALU.mult))
                chain(v.tensor_tensor(pos[:, 3, :], base[:, :], pos[:, 0, :], ALU.add))
                for m in range(2, -(-N // RING)):
                    chain(v.tensor_tensor(pos[:, 3, :], pos[:, 3, :], pos[:, m - 1, :], ALU.add))
                v.engine_nop().then_inc(prep, 1)
                dve.wait_ge(transposed, 5)
                chain(v.tensor_copy(pos_row[:, :], small_ps[0:1, 0:TC * P]))
                v.tensor_scalar(flag[:, :], out_ps[0:1, 0:1], 0.0, None, ALU.is_equal).then_inc(flag_ready, 1)
                v.tensor_copy(rel[:, :], banks[:, 1, 0:TC * P]).then_inc(tables, 1)
                chain(v.tensor_copy(wgt[:, :], banks[:, 2, 0:TC * P]))
                v.engine_nop().then_inc(tables, 1)
                v.tensor_copy(dstc[:, :], banks[:, 3, 0:TC * P]).then_inc(tables, 2)
                v.memset(sums[:, :, :], 0.0)
                dve.wait_ge(consts, 4)
                for j in range(1, Q):
                    chain(v.tensor_scalar(rel_of_part[:, j:j + 1], part_no[:, :], float(R * j), float(-R), ALU.is_ge, ALU.mult))
                chain(v.tensor_tensor(rel_of_part[:, 0:1], part_no[:, :], rel_of_part[:, 1:2], ALU.add))
                for j in range(2, Q):
                    chain(v.tensor_tensor(rel_of_part[:, 0:1], rel_of_part[:, 0:1], rel_of_part[:, j:j + 1], ALU.add))

                def coefs(n):
                    nt = min(QB * Q, QN * Q - n * QB * Q)
                    t0 = n * QB * Q
                    dve.wait_ge(coef_ps, n + 1)
                    v.tensor_tensor(coef[:, t0:t0 + nt, :], banks[:, 4 + n % 2, 0:nt * NB].rearrange("p (t b) -> p t b", b=NB),
                                    wgt[:, t0:t0 + nt].unsqueeze(2).to_broadcast([P, nt, NB]), ALU.mult).then_inc(coef_ready, 1)
                for n in range(NQB):
                    nq = min(QB, QN - n * QB)
                    if n == NQB - 1:
                        v.memset(et_i[:, n % 2, nq - 1, :], 0).then_inc(cleared, 1)
                    dve.wait_ge(et_in[n % 2], 16 * Q * (n // 2 + 1) + (16 if n == NQB - 1 else 0))
                    if n >= 2:
                        dve.wait_ge(coef_ps, n - 1)
                    v.tensor_scalar(et_hot[:, n % 2, 0:nq, :], et_i[:, n % 2, 0:nq, :], rel_of_part[:, 0:1], None,
                                    ALU.is_equal).then_inc(hot_ready, 1)
                    if n >= 1:
                        coefs(n - 1)
                coefs(NQB - 1)
                dve.wait_ge(coef_ready, NQB)

                ok = dve.value_load(flag[0:1, 0:1], min_val=0, max_val=1)
                with dve.If(ok == 1):
                    def window(t, s):
                        if not isinstance(t, int) or t >= MASKS:
                            dve.wait_ge(part_ready, t - MASKS + 1)
                        v.scalar_tensor_tensor(
                            win[:, s % MASKS, :, :],
                            node_iota[:, 0:WIN].unsqueeze(1).to_broadcast([P, NB, WIN]), rel[:, bass.ds(t, 1)],
                            coef[:, bass.ds(t, 1), :].rearrange("p o b -> p (o b)").unsqueeze(2).to_broadcast([P, NB, WIN]),
                            ALU.is_equal, ALU.mult).then_inc(win_ready, 1)

                    def add_part(t, s):
                        at = dve.value_load(pos_row[0:1, bass.ds(t, 1)], min_val=0, max_val=RING - 1)
                        dve.wait_ge(part_ready, t + 1)
                        if not isinstance(t, int) or t >= 1:
                            dve.wait_ge(part_added, t)
                        ring = sums[:, :, bass.ds(at, WIN)]
                        v.tensor_tensor(ring, ring, part[:, s % PARTS, :].rearrange("p (c n) -> p c n", n=WIN),
                                        ALU.add).then_inc(part_added, 1)

                    def fold(k, done):
                        if not isinstance(k, int) or k >= 1:
                            dve.wait_ge(cleaned, UNITS * k)
                        dve.wait_ge(part_added, done)
                        v.tensor_tensor(sums[:, :, 0:WIN], sums[:, :, 0:WIN], sums[:, :, RING:RING + WIN],
                                        ALU.add).then_inc(folded, 1)
                        dve.wait_ge(folded, 2 * k + 1)
                        v.memset(sums[:, :, RING:RING + WIN], 0.0).then_inc(folded, 1)

                    def norm(k, rows_k):
                        n0 = 6 * k
                        dve.wait_ge(block_done, k + 1)
                        dve.wait_ge(x_in, 16 * k + 16)
                        if not isinstance(k, int) or k >= 1:
                            dve.wait_ge(out_written, 16 * k)
                        v.tensor_tensor(y[rows_k, :], out_ps[rows_k, :], xres[rows_k, :], ALU.add).then_inc(evacuated, 1)
                        dve.wait_ge(evacuated, k + 2)
                        v.tensor_tensor(y[rows_k, :], y[rows_k, :], bias_all[rows_k, :], ALU.add).then_inc(norm_v, 1)
                        dve.wait_ge(norm_v, n0 + 1)
                        v.bn_stats(stats[rows_k, :], y[rows_k, :]).then_inc(norm_v, 1)
                        dve.wait_ge(norm_v, n0 + 2)
                        dve.sem_inc(dve_turns, 1)
                        v.bn_aggr(mv[rows_k, :], stats[rows_k, :]).then_inc(norm_v, 1)
                        dve.wait_ge(norm_a, 2 * k + 1)
                        v.reciprocal(sd[rows_k, 1:2], sd[rows_k, 0:1]).then_inc(norm_v, 1)
                        dve.wait_ge(norm_v, n0 + 4)
                        v.tensor_scalar(sd[rows_k, 2:3], mv[rows_k, 0:1], sd[rows_k, 1:2], -1.0, ALU.mult, ALU.mult).then_inc(norm_v, 2)

                    for t in range(AHEAD):
                        window(t, t)
                    for t in range(SLOTS):
                        window(t + AHEAD, t + AHEAD)
                        add_part(t, t)
                    with dve.Fori(1, HEAD // SLOTS) as g:
                        for s in range(SLOTS):
                            window(g * SLOTS + (s + AHEAD), s + AHEAD)
                            add_part(g * SLOTS + s, s)
                    with dve.Fori(0, NBLK - 2) as k:
                        fold(k, k * TPB + HEAD)
                        with dve.Fori(0, GPB) as g:
                            for s in range(SLOTS):
                                window(k * TPB + g * SLOTS + (HEAD + s + AHEAD), s + AHEAD)
                                add_part(k * TPB + g * SLOTS + (HEAD + s), s)
                        norm(k, slice(0, BLK))
                    fold(NBLK - 2, TAIL)
                    for t in range(TAIL, T):
                        if t + AHEAD < T:
                            window(t + AHEAD, t + AHEAD)
                        add_part(t, t)
                    fold(NBLK - 1, T)
                    norm(NBLK - 2, slice(0, BLK))
                    norm(NBLK - 1, slice(0, N - (NBLK - 1) * BLK))
                with dve.Else():
                    gr = slice(0, GEN_NODES)
                    v.engine_nop().then_inc(g_sum, 1)
                    with dve.Fori(0, N // GEN_NODES) as w:
                        with dve.Fori(0, T) as t:
                            dve.wait_ge(g_step, w * T + t + 1)
                            v.scalar_tensor_tensor(
                                gwin[:, :, :], node_iota[:, :].unsqueeze(1).to_broadcast([P, NB, GEN_NODES]),
                                dstc[:, bass.ds(t, 1)],
                                coef[:, bass.ds(t, 1), :].rearrange("p o b -> p (o b)").unsqueeze(2).to_broadcast([P, NB, GEN_NODES]),
                                ALU.is_equal, ALU.mult).then_inc(g_win, 1)
                        dve.wait_ge(g_mm, w * T + T)
                        for c in range(IC):
                            g = v.tensor_copy(gsum[:, c, :, :], banks[:, c, 0:NB * GEN_NODES].rearrange("p (b n) -> p b n", b=NB))
                        v.tensor_scalar(dstc[:, :], dstc[:, :], float(-GEN_NODES), None, ALU.add).then_inc(g_sum, 1)
                        dve.wait_ge(g_sum, w + 2)
                        dve.sem_inc(g_out, 1)
                        dve.wait_ge(block_done, w + 1)
                        dve.wait_ge(g_x, 16 * w + 16)
                        v.tensor_tensor(y[gr, :], out_ps[gr, :], xres[gr, :], ALU.add).then_inc(g_v, 1)
                        dve.wait_ge(g_v, 6 * w + 1)
                        v.tensor_tensor(y[gr, :], y[gr, :], bias_all[gr, :], ALU.add).then_inc(g_v, 1)
                        dve.wait_ge(g_v, 6 * w + 2)
                        v.bn_stats(stats[gr, :], y[gr, :]).then_inc(g_v, 1)
                        dve.wait_ge(g_v, 6 * w + 3)
                        dve.sem_inc(dve_turns, 1)
                        v.bn_aggr(mv[gr, :], stats[gr, :]).then_inc(g_v, 1)
                        dve.wait_ge(g_a, 2 * w + 1)
                        v.reciprocal(sd[gr, 1:2], sd[gr, 0:1]).then_inc(g_v, 1)
                        dve.wait_ge(g_v, 6 * w + 5)
                        v.tensor_scalar(sd[gr, 2:3], mv[gr, 0:1], sd[gr, 1:2], -1.0, ALU.mult, ALU.mult).then_inc(g_v, 1)
                        dve.wait_ge(g_w, 16 * w + 16)

            @block.scalar
            def _(act):
                a = nc.scalar
                act.wait_ge(flag_ready, 1)
                act.sem_inc(unit_free, 2)
                act.sem_inc(evacuated, 1)
                ok = act.value_load(flag[0:1, 0:1], min_val=0, max_val=1)
                with act.If(ok == 1):
                    def unit_copy(k, u):
                        act.wait_ge(unit_free, k * UNITS + u + 1)
                        if u == 0:
                            act.wait_ge(folded, 2 * k + 2)
                        act.sem_inc(act_turns, 1)
                        planes = sums[:, u * UNIT:(u + 1) * UNIT, bass.ds(k % RING_BLOCKS * BLK, BLK)]
                        a.activation(unit[:, u % 2, :, :], planes, ACT.Copy).then_inc(unit_ready, 1)
                        act.wait_ge(unit_ready, k * UNITS + u + 1)
                        act.sem_inc(act_turns, 1)
                        a.activation(planes, zero[:, 0:1].unsqueeze(2).to_broadcast([P, UNIT, BLK]), ACT.Copy).then_inc(cleaned, 1)

                    def finish(k, rows_k, out_k):
                        act.wait_ge(norm_v, 6 * k + 3)
                        a.activation(sd[rows_k, 0:1], mv[rows_k, 1:2], ACT.Sqrt, bias=eps[rows_k, 0:1]).then_inc(norm_a, 1)
                        act.wait_ge(norm_v, 6 * k + 6)
                        a.activation(y[rows_k, :], y[rows_k, :], ACT.Identity, bias=sd[rows_k, 2:3],
                                     scale=sd[rows_k, 1:2]).then_inc(norm_a, 1)
                        act.wait_ge(norm_a, 2 * k + 2)
                        act.dma_start(out_k, y[rows_k, :]).then_inc(out_written, 16)

                    with act.Fori(0, NBLK - 2) as k:
                        act.wait_ge(evacuated, k + 1)
                        act.dma_start(xres[:, :], x[bass.ds(k * BLK, BLK), :]).then_inc(x_in, 16)
                        for u in range(UNITS):
                            unit_copy(k, u)
                        finish(k, slice(0, BLK), out[bass.ds(k * BLK, BLK), :])
                    for k in (NBLK - 2, NBLK - 1):
                        n = min(BLK, N - k * BLK)
                        act.wait_ge(evacuated, k + 1)
                        act.dma_start(xres[0:n, :], x[k * BLK:k * BLK + n, :]).then_inc(x_in, 16)
                        for u in range(UNITS):
                            unit_copy(k, u)
                        finish(k, slice(0, n), out[k * BLK:k * BLK + n, :])
                    act.wait_ge(out_written, 16 * NBLK)
                with act.Else():
                    gr = slice(0, GEN_NODES)
                    for s in range(SLOTS):
                        act.wait_ge(row_in[s], 16)
                    with act.Fori(0, N // GEN_NODES) as w:
                        act.dma_start(xres[gr, :], x[bass.ds(w * GEN_NODES, GEN_NODES), :]).then_inc(g_x, 16)

                        def step(i, t):
                            a.copy(gidx[:, 0:1], idx[:, bass.ds(t, 1)]).then_inc(g_idx, 1)
                            act.sem_inc(g_step, 1)
                            act.wait_ge(g_mm, i + 1)
                        with act.Fori(0, T) as t:
                            step(w * T + t, t)
                        act.wait_ge(g_v, 6 * w + 4)
                        a.activation(sd[gr, 0:1], mv[gr, 1:2], ACT.Sqrt, bias=eps[gr, 0:1]).then_inc(g_a, 1)
                        act.wait_ge(g_v, 6 * w + 6)
                        a.activation(y[gr, :], y[gr, :], ACT.Identity, bias=sd[gr, 2:3], scale=sd[gr, 1:2]).then_inc(g_a, 1)
                        act.wait_ge(g_a, 2 * w + 2)
                        act.dma_start(out[bass.ds(w * GEN_NODES, GEN_NODES), :], y[gr, :]).then_inc(g_w, 16)
                        act.wait_ge(g_w, 16 * w + 16)


_INS = ["x", "src", "dst", "edge_type_32", "edge_weight1", "L0_gnn_bases", "L0_gnn_w_comp", "L0_gnn_h_bias"]


def kernel(**inputs):
    import numpy as np
    import concourse.bacc as bacc
    from concourse import mybir
    from concourse.bass_utils import run_bass_kernel_spmd

    nc = bacc.Bacc("TRN2", target_bir_lowering=False, num_devices=1)
    arrays, args = {}, []
    for name in _INS:
        a = np.ascontiguousarray(inputs[name])
        arrays[f"in_{name}"] = a
        args.append(nc.dram_tensor(f"in_{name}", a.shape, mybir.dt.from_np(a.dtype), kind="ExternalInput").ap())
    args.append(nc.dram_tensor("out", inputs["x"].shape, mybir.dt.float32, kind="ExternalOutput").ap())
    rgcn_resnorm(nc, *args)
    r = run_bass_kernel_spmd(nc, [arrays], core_ids=[0])
    return r.results[0]["out"]
```

```python
from contextlib import ExitStack

import concourse.bass as bass
from concourse import mybir

ALU = mybir.AluOpType
ACT = mybir.ActivationFunctionType
AX_X = mybir.AxisListType.X
F32 = mybir.dt.float32
I32 = mybir.dt.int32
U32 = mybir.dt.uint32
BF16 = mybir.dt.bfloat16
F32R = mybir.dt.float32r

P = 128
EPS = 1e-5
WIN = 8
BLK = P
HALF = BLK // 2
RING = 5 * HALF
SLOTS = 8
LATE = 8
EARLY = 8
PARTS = 4
UNIT = 4
LAG = 4
SPLIT = 2
GEN = 50
POOL_PLANES = 16


def rgcn_resnorm(nc, x, src, dst, etype, weight, bases, w_comp, h_bias, out):
    N, F = x.shape
    E = src.shape[0]
    R, NB = w_comp.shape
    T = -(-E // P)
    LAST = E - (T - 1) * P
    TC = -(-T // P)
    IC = F // P
    PL = IC * NB
    NBLK = -(-N // BLK)
    TPB = E * BLK // (N * P)
    NPT = BLK // TPB
    UNITS = PL // UNIT
    CUNITS = NB // UNIT
    LOWS = SPLIT * CUNITS
    HEAD = TPB + LATE
    GPB = TPB // SLOTS
    NG = -(-T // SLOTS)
    TAIL = HEAD + (NBLK - 2) * TPB
    PAIRS = (HEAD // SLOTS - 1) // 2
    SPW = SPLIT * NB // PAIRS
    Q = P // R
    SB = 4
    BT = SB * Q
    QN = -(-T // Q)
    NSB = -(-QN // SB)
    PRE = 4
    assert E * BLK == TPB * N * P and LAST * 2 == P and NG % 2 == 0 and T == (NG - 1) * SLOTS + 1
    assert HEAD == SLOTS * (1 + 2 * PAIRS) and PL == TPB and N % GEN == 0 and SPW % 2 == 0
    assert NPT * (TPB * 2 - 1 + HEAD - TPB + EARLY) - RING < BLK + NPT * LATE

    with ExitStack() as ctx:
        def sb(name, shape, dt=F32, stack=ctx):
            return stack.enter_context(nc.sbuf_tensor(name, shape, dt))

        def psum(name, shape):
            return ctx.enter_context(nc.psum_tensor(name, shape, F32))

        def sem(name):
            return ctx.enter_context(nc.semaphore(name))

        rows = sb("rows", [P, SLOTS, F])
        sums = sb("sums", [P, PL, RING + WIN])
        hot8 = sb("hot8", [P, 2, SLOTS, WIN])
        win = sb("win", [P, 2, SLOTS, NB, WIN])
        unit_f = sb("unit_f", [P, 2, UNIT, BLK])
        unit_h = sb("unit_h", [P, 2, UNIT, BLK], F32R)
        unit_l = sb("unit_l", [P, 2, UNIT, BLK], F32R)
        xres = sb("xres", [P, F])
        y = sb("y", [P, F])
        stats = sb("stats", [P, 6])
        mv = sb("mv", [P, 2])
        sd = sb("sd", [P, 4])
        bases_h = sb("bases_h", [P, SPLIT * NB, F], F32R)
        bases_l = sb("bases_l", [P, SPLIT * NB, F], F32R)
        bases_f = sb("bases_f", [P, (IC - SPLIT) * NB, F])
        idx = sb("idx", [P, TC * P], U32)
        rel = sb("rel", [P, TC * P])
        dstc = sb("dstc", [P, TC * P])
        wgt = sb("wgt", [P, TC * P])
        coef = sb("coef", [P, NSB * BT, NB])
        idx_s = sb("idx_s", [P, 2, SLOTS], U32)
        pos_row = sb("pos_row", [1, TC * P], I32)
        flag = sb("flag", [1, 1], I32)
        ident = sb("ident", [P, P])
        ones = sb("ones", [P, 1])
        zero = sb("zero", [P, 1])
        eps = sb("eps", [P, 1])
        node_iota = sb("node_iota", [P, GEN])
        part_no = sb("part_no", [P, 1])
        rel_of_part = sb("rel_of_part", [P, Q])
        tile_nodes = sb("tile_nodes", [P, TC])
        bias_all = sb("bias_all", [P, F])
        w_diag = sb("w_diag", [P, Q * NB])
        w_part = sb("w_part", [P, 3, Q * NB], BF16)
        w_rest = sb("w_rest", [P, 2, Q * NB])
        et_b = sb("et_b", [P, TC, P], BF16)
        et_all = sb("et_all", [P, 2, SB, P], BF16)
        et_hot = sb("et_hot", [P, 2, SB, P], BF16)
        base = sb("base", [P, TC])
        top = sb("top", [P, TC])
        chk = sb("chk", [P, 4, TC])
        bad = sb("bad", [P, 1])
        pos = sb("pos", [P, 4, TC])
        rel_f = sb("rel_f", [P, TC, P])
        wgt_t = sb("wgt_t", [P, TC, P])
        dst_f = sb("dst_f", [P, TC, P])
        flat_win = [win[:, g, :, :, :].rearrange("p t b n -> p (t b n)") for g in range(2)]
        flat_unit = unit_f[:, :, :, :].rearrange("p g j n -> p (g j n)")

        def early(flat, at=0):
            return flat[:, at:at + TC * P].rearrange("p (c e) -> p c e", e=P)
        src_f = early(flat_win[0])
        pick = bases_f[:, 0:P * R // (2 * F), :].rearrange("p b f -> p (b f)").bitcast(BF16)
        src_i = early(flat_unit).bitcast(I32)
        et_i = early(flat_unit, TC * P).bitcast(I32)
        dst_i = early(flat_win[1]).bitcast(I32)
        gidx = idx_s[:, 0, 0:2]
        gwin = win[:, :, :, :, :].rearrange("p g t b n -> p (g t b n)")[:, 0:NB * GEN].rearrange("p (b n) -> p b n", b=NB)
        gsum = sums[:, :, 0:GEN]
        banks = psum("banks", [P, 8, 512])
        part = banks[:, 0:PARTS, 0:PL * WIN]
        type_ps = banks[:, 4, :]
        coef_bank = banks[:, 5, :]
        out_ps = banks[:, 6, :]
        small_ps = banks[:, 7, :]

        src_in, dst_in, et_in, wgt_in = sem("src_in"), sem("dst_in"), sem("et_in"), sem("wgt_in")
        const_in = sem("const_in")
        basesf_in = [sem(f"basesf_in{c}") for c in range(IC - SPLIT)]
        raw_in = [sem("raw_in0"), sem("raw_in1")]
        high_ready, low_ready = sem("high_ready"), sem("low_ready")
        consts, pool_c, swept = sem("consts"), sem("pool_c"), sem("swept")
        cleared, prep, chained, picked = sem("cleared"), sem("prep"), sem("chained"), sem("picked")
        transposed, tables = sem("transposed"), sem("tables")
        type_done, type_copied, hot_ready, coef_done, coef_ready = (
            sem("type_done"), sem("type_copied"), sem("hot_ready"), sem("coef_done"), sem("coef_ready"))
        row_in = [sem(f"row_in{s}") for s in range(SLOTS)]
        idx_in = [sem("idx_in0"), sem("idx_in1")]
        flag_ready = sem("flag_ready")
        turns, dve_turns, act_turns = sem("turns"), sem("dve_turns"), sem("act_turns")
        hot8_ready, win_ready, part_ready, part_added = (
            sem("hot8_ready"), sem("win_ready"), sem("part_ready"), sem("part_added"))
        folded, unit_copied, unit_split, unit_free = sem("folded"), sem("unit_copied"), sem("unit_split"), sem("unit_free")
        cleaned = sem("cleaned")
        block_done, evacuated = sem("block_done"), sem("evacuated")
        x_in, out_written = sem("x_in"), sem("out_written")
        norm_v, norm_a = sem("norm_v"), sem("norm_a")
        g_step, g_idx, g_win, g_mm = sem("g_step"), sem("g_idx"), sem("g_win"), sem("g_mm")
        g_row = [sem("g_row0"), sem("g_row1")]
        g_base = [sem(f"g_base{i}") for i in range(4)]
        g_used, g_done = sem("g_used"), sem("g_done")
        g_sum, g_out, g_v, g_a, g_x, g_w = sem("g_sum"), sem("g_out"), sem("g_v"), sem("g_a"), sem("g_x"), sem("g_w")

        TL = T - (TC - 1) * P
        full = (TC - 1) * P * P

        def half_pieces(k, start, size):
            return (k * BLK + start) % RING

        with nc.Block() as block:

            @block.sync
            def _(sp):
                for n, (a, t, s) in enumerate(((src, src_i, src_in), (dst, dst_i, dst_in), (etype, et_i, et_in),
                                               (weight.rearrange("e o -> (e o)"), wgt_t, wgt_in))):
                    sp.dma_start(t[:, 0:TC - 1, :], a[0:full].rearrange("(c p e) -> p c e", p=P, e=P)).then_inc(s, 16)
                    sp.wait_ge(cleared, n + 1)
                    sp.dma_start(t[0:TL - 1, TC - 1, :], a[full:full + (TL - 1) * P].rearrange("(p e) -> p e", e=P)).then_inc(s, 16)
                    half = a[E - LAST:E].unsqueeze(0)
                    sp.dma_start(t[TL - 1:TL, TC - 1, 0:LAST], half).then_inc(s, 16)
                    if n < 3:
                        sp.dma_start(t[TL - 1:TL, TC - 1, LAST:P], half).then_inc(s, 16)
                sp.wait_ge(cleared, 5)
                for j in range(Q):
                    sp.dma_start(w_diag[R * j:R * j + R, NB * j:NB * j + NB], w_comp).then_inc(const_in, 16)
                sp.dma_start(bias_all[:, :], h_bias.partition_broadcast(P)).then_inc(const_in, 16)
                sp.wait_ge(flag_ready, 1)
                ok = sp.value_load(flag[0:1, 0:1], min_val=0, max_val=1)
                with sp.If(ok == 1):
                    def stage(g, par, wait):
                        if wait is not None:
                            sp.wait_ge(row_in[SLOTS - 1], wait)
                        sp.dma_start(idx_s[:, par, :], idx[:, bass.ds(g * SLOTS, SLOTS)]).then_inc(idx_in[par], 16)
                    stage(1, 1, None)
                    with sp.Fori(1, NG // 2) as h:
                        stage(2 * h, 0, 32 * h - 16)
                        stage(2 * h + 1, 1, 32 * h)
                with sp.Else():
                    with sp.Fori(0, N // GEN) as w:
                        for p in range(SPLIT * NB):
                            sp.wait_ge(g_used, w * (SPLIT * NB) + p + 1)
                            sp.dma_start(rows[:, 4 + p % 4, :], bases[p % NB, p // NB * P:(p // NB + 1) * P, :]).then_inc(g_base[p % 4], 16)

            @block.gpsimd
            def _(pool):
                nc.gpsimd.memset(ident[:, :], 0.0).then_inc(pool_c, 1)
                pool.wait_ge(pool_c, 1)
                nc.gpsimd.affine_select(out=ident[:, :], in_=ident[:, :], compare_op=ALU.not_equal, fill=1.0,
                                        base=0, pattern=[[-1, P]], channel_multiplier=1).then_inc(consts, 1)
                nc.gpsimd.iota(node_iota[:, :], [[1, GEN]], base=0, channel_multiplier=0,
                               allow_small_or_imprecise_dtypes=True).then_inc(consts, 1)
                nc.gpsimd.iota(tile_nodes[:, :], [[NPT * P, TC]], base=0, channel_multiplier=NPT,
                               allow_small_or_imprecise_dtypes=True).then_inc(consts, 1)
                nc.gpsimd.iota(part_no[:, :], [[1, 1]], base=0, channel_multiplier=1,
                               allow_small_or_imprecise_dtypes=True).then_inc(consts, 1)
                nc.gpsimd.memset(sums[:, 0:POOL_PLANES, :], 0.0).then_inc(swept, 1)

                def gather(s, index):
                    return pool.indirect_dma_start(rows[:, s, :], None, x, bass.IndirectOffsetOnAxis(index, 0))

                pool.wait_ge(tables, 1)
                for s in range(SLOTS):
                    gather(s, idx[:, s:s + 1]).then_inc(row_in[s], 16)
                pool.wait_ge(flag_ready, 1)
                ok = pool.value_load(flag[0:1, 0:1], min_val=0, max_val=1)
                with pool.If(ok == 1):
                    def group(par, idx_wait, first_tile, slots=SLOTS):
                        pool.wait_ge(idx_in[par], idx_wait)
                        pool.sem_inc(turns, 1)
                        for s in range(slots):
                            pool.wait_ge(part_ready, first_tile + s - SLOTS + 1)
                            pool.sem_inc(turns, 1)
                            gather(s, idx_s[:, par, s:s + 1]).then_inc(row_in[s], 16)
                    group(1, 16, SLOTS)
                    with pool.Fori(1, NG // 2 - 1) as h:
                        group(0, 16 * h, 2 * SLOTS * h)
                        group(1, 16 * h + 16, 2 * SLOTS * h + SLOTS)
                    h = NG // 2 - 1
                    group(0, 16 * h, 2 * SLOTS * h)
                    group(1, 16 * h + 16, 2 * SLOTS * h + SLOTS, 1)
                with pool.Else():
                    for s in range(SLOTS):
                        pool.wait_ge(row_in[s], 16)

                    def general(i, b):
                        pool.wait_ge(g_idx, i + 1)
                        pool.sem_inc(turns, 1)
                        gather(b, gidx[:, b:b + 1]).then_inc(g_row[b], 16)
                    with pool.Fori(0, N // GEN) as w:
                        with pool.Fori(0, T // 2) as h:
                            general(w * T + 2 * h, 0)
                            general(w * T + 2 * h + 1, 1)
                        general(w * T + T - 1, 0)

            @block.tensor
            def _(pe):
                pe.wait_ge(consts, 1)

                def table(n, a, s, v):
                    pe.wait_ge(s, v)
                    for c in range(TC):
                        m = nc.tensor.transpose(banks[:, n, c * P:(c + 1) * P], a[:, c, :], ident[:, :])
                    m.then_inc(transposed, 1)

                def types(i):
                    pe.wait_ge(hot_ready, 1)
                    pe.wait_ge(picked, 1)
                    if i >= 1:
                        pe.wait_ge(type_copied, i)
                    for q in range(i * SB, min(QN, i * SB + SB)):
                        c, t = q * Q // P, q * Q % P
                        m = nc.tensor.matmul(type_ps[:, (q - i * SB) * P:(q - i * SB + 1) * P],
                                             pick[:, t * R:(t + Q) * R], et_b[:, c, :],
                                             start=True, stop=True)
                    m.then_inc(type_done, 1)

                def coefs(i):
                    if i + 1 < NSB:
                        types(i + 1)
                    pe.wait_ge(hot_ready, i + 2)
                    if i >= 1:
                        pe.wait_ge(coef_ready, i)
                    nq = min(SB, QN - i * SB)
                    for q in range(nq):
                        for w in range(3):
                            m = nc.tensor.matmul(coef_bank[:, q * Q * NB:(q + 1) * Q * NB], et_hot[:, i % 2, q, :],
                                                 w_part[:, w, :], start=(w == 0), stop=(w == 2))
                    m.then_inc(coef_done, 1)

                table(0, src_f, prep, 1)
                table(1, rel_f, prep, 2)
                types(0)
                table(2, wgt_t, wgt_in, 48)
                pe.wait_ge(prep, 3)
                for c in range(TC):
                    nc.tensor.transpose(small_ps[0:1, c * P:(c + 1) * P], pos[:, 3, c:c + 1], ident[:, :])
                nc.tensor.matmul(out_ps[0:1, 0:1], bad[:, 0:1], ones[:, 0:1], start=True, stop=True).then_inc(transposed, 1)
                table(3, dst_f, prep, 3)
                for i in range(PRE):
                    coefs(i)
                pe.wait_ge(tables, 4)
                pe.wait_ge(flag_ready, 1)
                ok = pe.value_load(flag[0:1, 0:1], min_val=0, max_val=1)
                with pe.If(ok == 1):
                    def tile_product(t, s, par, row_wait, win_wait):
                        pe.wait_ge(row_in[s], row_wait)
                        if s == 0:
                            pe.wait_ge(win_ready, win_wait)
                        pe.wait_ge(part_added, t - PARTS + 2 if not isinstance(t, int) or t >= PARTS else 1)
                        for c in range(IC):
                            m = nc.tensor.matmul(part[:, s % PARTS, c * NB * WIN:(c + 1) * NB * WIN],
                                                 rows[:, s, c * P:(c + 1) * P], win[:, par, s, :, :],
                                                 start=True, stop=True)
                        m.then_inc(part_ready, 1)

                    def plane_product(k, p):
                        u, j, b = p // UNIT, p % UNIT, p // UNIT % 2
                        if p == 0:
                            pe.wait_ge(evacuated, k + 1)
                        first, last = p == 0, p == PL - 1
                        if p < SPLIT * NB:
                            if j == 0:
                                pe.wait_ge(unit_split, k * LOWS + u + 1)
                            nc.tensor.matmul(out_ps, unit_h[:, b, j, :], bases_h[:, p, :], start=first, stop=False)
                            nc.tensor.matmul(out_ps, unit_l[:, b, j, :], bases_h[:, p, :], start=False, stop=False)
                            m = nc.tensor.matmul(out_ps, unit_h[:, b, j, :], bases_l[:, p, :], start=False, stop=last)
                        else:
                            if j == 0:
                                pe.wait_ge(unit_copied, k * UNITS + u + 1)
                            m = nc.tensor.matmul(out_ps, unit_f[:, b, j, :], bases_f[:, p - SPLIT * NB, :], start=first, stop=last)
                        if last:
                            m.then_inc(block_done, 1)
                        elif j == UNIT - 1:
                            m.then_inc(unit_free, 1)

                    for s in range(SLOTS):
                        for i in range(PRE + 2 * s, min(NSB, PRE + 2 * s + 2)):
                            coefs(i)
                        tile_product(s, s, 0, 16, 1)
                    with pe.Fori(0, PAIRS) as h:
                        for s in range(2 * SLOTS):
                            g = s // SLOTS + 1
                            tile_product(h * (2 * SLOTS) + (SLOTS + s), s % SLOTS, g % 2, h * 32 + 16 * (g + 1), h * 2 + (g + 1))
                    for c in range(IC - SPLIT):
                        pe.wait_ge(basesf_in[c], 16)
                    pe.wait_ge(low_ready, SPLIT * NB)
                    with pe.Fori(0, NBLK - 2) as k:
                        for p in range(PL):
                            g = (HEAD + p) // SLOTS
                            tile_product(k * TPB + (HEAD + p), p % SLOTS, g % 2, k * (GPB * 16) + (g * 16 + 16), k * GPB + (g + 1))
                            if p >= LAG:
                                plane_product(k, p - LAG)
                        for p in range(PL - LAG, PL):
                            plane_product(k, p)
                    for p in range(PL + LAG):
                        t = TAIL + p
                        if t < T:
                            g = t // SLOTS
                            tile_product(t, t % SLOTS, g % 2, g * 16 + 16, g + 1)
                        if p >= LAG:
                            plane_product(NBLK - 2, p - LAG)
                    for p in range(PL):
                        plane_product(NBLK - 1, p)
                with pe.Else():
                    for i in range(PRE, NSB):
                        coefs(i)
                    for c in range(IC - SPLIT):
                        pe.wait_ge(basesf_in[c], 16)
                    with pe.Fori(0, N // GEN) as w:
                        def product(i, b, row_wait, first):
                            pe.wait_ge(g_row[b], row_wait)
                            pe.wait_ge(g_win, i + 1)
                            for c in range(IC):
                                m = nc.tensor.matmul(banks[:, c, 0:NB * GEN], rows[:, b, c * P:(c + 1) * P],
                                                     gwin[:, :, :], start=first, stop=False, skip_group_check=True)
                            m.then_inc(g_mm, 1)
                        pe.wait_ge(g_sum, w + 1)
                        product(w * T, 0, 16 * (T // 2 + 1) * w + 16, True)
                        product(w * T + 1, 1, 16 * (T // 2) * w + 16, False)
                        with pe.Fori(1, T // 2) as h:
                            product(w * T + 2 * h, 0, 16 * (T // 2 + 1) * w + 16 * h + 16, False)
                            product(w * T + 2 * h + 1, 1, 16 * (T // 2) * w + 16 * h + 16, False)
                        product(w * T + T - 1, 0, 16 * (T // 2 + 1) * w + 16 * (T // 2 + 1), False)
                        pe.wait_ge(g_sum, w + 2)
                        pe.wait_ge(g_out, w + 1)
                        for p in range(PL):
                            if p < SPLIT * NB:
                                pe.wait_ge(g_base[p % 4], 16 * (SPLIT * NB // 4) * w + 16 * (p // 4) + 16)
                                right = rows[:, 4 + p % 4, :]
                            else:
                                right = bases_f[:, p - SPLIT * NB, :]
                            m = nc.tensor.matmul(out_ps[0:GEN, :], gsum[:, p, :], right, start=(p == 0), stop=(p == PL - 1))
                            if p < SPLIT * NB:
                                m.then_inc(g_used, 1)
                        m.then_inc(g_done, 1)

            @block.vector
            def _(dve):
                v = nc.vector
                n_chain = [0]

                def chain(ins):
                    n_chain[0] += 1
                    ins.then_inc(chained, 1)
                    dve.wait_ge(chained, n_chain[0])

                v.memset(zero[:, :], 0.0).then_inc(swept, 1)
                for a in (src_i, dst_i, et_i):
                    v.memset(a[:, TC - 1, :], 0).then_inc(cleared, 1)
                v.memset(wgt_t[:, TC - 1, :], 0.0).then_inc(cleared, 1)
                v.memset(w_diag[:, :], 0.0).then_inc(cleared, 1)
                v.memset(ones[:, :], 1.0)
                v.memset(eps[:, :], EPS)
                dve.wait_ge(src_in, 64)
                v.tensor_copy(src_f, src_i[:, :, :]).then_inc(prep, 1)
                dve.wait_ge(consts, 4)
                for j in range(1, Q):
                    r = v.tensor_scalar(rel_of_part[:, j:j + 1], part_no[:, :], float(R * j), float(-R), ALU.is_ge, ALU.mult)
                chain(r)
                dve.wait_ge(transposed, 1)
                v.tensor_copy(idx[:, :], banks[:, 0, 0:TC * P]).then_inc(tables, 1)
                chain(v.tensor_tensor(rel_of_part[:, 0:1], part_no[:, :], rel_of_part[:, 1:2], ALU.add))
                for j in range(2, Q):
                    chain(v.tensor_tensor(rel_of_part[:, 0:1], rel_of_part[:, 0:1], rel_of_part[:, j:j + 1], ALU.add))
                dve.wait_ge(dst_in, 64)
                chain(v.tensor_copy(dst_f[:, :, :], dst_i[:, :, :]))
                v.tensor_reduce(base[:, :], dst_f[:, :, :], AX_X, ALU.min)
                chain(v.tensor_reduce(top[:, :], dst_f[:, :, :], AX_X, ALU.max))
                v.tensor_tensor(rel_f[:, :, :], dst_f[:, :, :], base[:, :].unsqueeze(2).to_broadcast([P, TC, P]),
                                ALU.subtract).then_inc(prep, 1)
                dve.wait_ge(et_in, 64)
                v.tensor_copy(et_b[:, :, :], et_i[:, :, :]).then_inc(hot_ready, 1)
                v.tensor_tensor(chk[:, 0, :], top[:, :], base[:, :], ALU.subtract)
                v.tensor_tensor(chk[:, 1, :], tile_nodes[:, :], base[:, :], ALU.subtract)
                chain(v.tensor_tensor(chk[:, 2, :], top[:, :], tile_nodes[:, :], ALU.subtract))
                v.tensor_scalar(chk[:, 0, :], chk[:, 0, :], float(WIN), None, ALU.is_ge)
                v.tensor_scalar(chk[:, 1, :], chk[:, 1, :], float(NPT * LATE), None, ALU.is_gt)
                v.tensor_scalar(chk[:, 2, :], chk[:, 2, :], float(NPT * EARLY), None, ALU.is_gt)
                for m in range(1, 4):
                    r = v.tensor_scalar(pos[:, m - 1, :], base[:, :], float(m * RING), float(-RING), ALU.is_ge, ALU.mult)
                chain(r)
                v.tensor_tensor(chk[:, 0, :], chk[:, 0, :], chk[:, 1, :], ALU.add)
                v.tensor_tensor(pos[:, 0, :], pos[:, 0, :], pos[:, 1, :], ALU.add)
                chain(v.tensor_tensor(pos[:, 2, :], pos[:, 2, :], base[:, :], ALU.add))
                v.tensor_tensor(pos[:, 3, :], pos[:, 0, :], pos[:, 2, :], ALU.add)
                chain(v.tensor_tensor(chk[:, 3, :], chk[:, 0, :], chk[:, 2, :], ALU.add))
                chain(v.tensor_reduce(bad[:, :], chk[:, 3, 0:TC - 1], AX_X, ALU.add))
                v.tensor_tensor(bad[0:TL, :], bad[0:TL, :], chk[0:TL, 3, TC - 1:TC], ALU.add).then_inc(prep, 1)
                dve.wait_ge(const_in, 16 * (Q + 1))
                chain(v.tensor_copy(w_part[:, 0, :], w_diag[:, :]))
                chain(v.tensor_tensor(w_rest[:, 0, :], w_diag[:, :], w_part[:, 0, :], ALU.subtract))
                chain(v.tensor_copy(w_part[:, 1, :], w_rest[:, 0, :]))
                chain(v.tensor_tensor(w_rest[:, 1, :], w_rest[:, 0, :], w_part[:, 1, :], ALU.subtract))
                chain(v.tensor_copy(w_part[:, 2, :], w_rest[:, 1, :]))
                dve.wait_ge(transposed, 4)
                v.tensor_copy(pos_row[:, :], small_ps[0:1, 0:TC * P]).then_inc(chained, 1)
                n_chain[0] += 1
                v.tensor_scalar(flag[:, :], out_ps[0:1, 0:1], 0.0, None, ALU.is_equal).then_inc(flag_ready, 1)
                v.tensor_copy(rel[:, :], banks[:, 1, 0:TC * P]).then_inc(tables, 1)
                v.tensor_copy(wgt[:, :], banks[:, 2, 0:TC * P]).then_inc(tables, 1)

                def hot(i):
                    nq = min(SB, QN - i * SB)
                    dve.wait_ge(type_copied, i + 1)
                    if i >= 2:
                        dve.wait_ge(coef_done, i - 1)
                    v.tensor_scalar(et_hot[:, i % 2, 0:nq, :], et_all[:, i % 2, 0:nq, :], rel_of_part[:, 0:1], None,
                                    ALU.is_equal).then_inc(hot_ready, 1)

                def coefs(i):
                    if i + 1 < NSB:
                        hot(i + 1)
                    nt = min(BT, QN * Q - i * BT)
                    dve.wait_ge(coef_done, i + 1)
                    v.tensor_tensor(coef[:, i * BT:i * BT + nt, :], coef_bank[:, 0:nt * NB].rearrange("p (t b) -> p t b", b=NB),
                                    wgt[:, i * BT:i * BT + nt].unsqueeze(2).to_broadcast([P, nt, NB]), ALU.mult).then_inc(coef_ready, 1)
                dve.wait_ge(tables, 3)
                hot(0)
                for i in range(PRE):
                    coefs(i)
                dve.wait_ge(transposed, 5)
                v.tensor_copy(dstc[:, :], banks[:, 3, 0:TC * P]).then_inc(tables, 1)
                dve.wait_ge(coef_ready, PRE)
                dve.wait_ge(swept, 3)

                ok = dve.value_load(flag[0:1, 0:1], min_val=0, max_val=1)
                with dve.If(ok == 1):
                    at = [dve.alloc_register(f"at{s}") for s in range(SLOTS)]

                    def window(g, par, n=SLOTS):
                        if not isinstance(g, int) or g >= 2:
                            dve.wait_ge(part_ready, g * SLOTS - SLOTS)
                        v.tensor_tensor(hot8[:, par, 0:n, :], rel[:, bass.ds(g * SLOTS, n)].unsqueeze(2).to_broadcast([P, n, WIN]),
                                        node_iota[:, 0:WIN].unsqueeze(1).to_broadcast([P, n, WIN]), ALU.is_equal).then_inc(hot8_ready, 1)
                        dve.wait_ge(hot8_ready, g + 1)
                        v.tensor_tensor(win[:, par, 0:n, :, :],
                                        coef[:, bass.ds(g * SLOTS, n), :].unsqueeze(3).to_broadcast([P, n, NB, WIN]),
                                        hot8[:, par, 0:n, :].unsqueeze(2).to_broadcast([P, n, NB, WIN]), ALU.mult).then_inc(win_ready, 1)

                    def positions(t, n=SLOTS):
                        dve.load(at[0:n], pos_row[0:1, bass.ds(t, n)])
                        return [dve.snap(r, min_val=0, max_val=RING - 1) for r in at[0:n]]

                    def add_part(t, s, where):
                        dve.wait_ge(part_ready, t + 1)
                        dve.wait_ge(part_added, t + 1)
                        ring = sums[:, :, bass.ds(where[s % SLOTS], WIN)]
                        v.tensor_tensor(ring, ring, part[:, s % PARTS, :].rearrange("p (c n) -> p c n", n=WIN),
                                        ALU.add).then_inc(part_added, 1)

                    def fold(k, done):
                        if not isinstance(k, int) or k >= 1:
                            dve.wait_ge(cleaned, UNITS * k)
                        dve.wait_ge(part_added, done + 1)
                        v.tensor_tensor(sums[:, :, 0:WIN], sums[:, :, 0:WIN], sums[:, :, RING:RING + WIN],
                                        ALU.add).then_inc(folded, 1)
                        dve.wait_ge(folded, 2 * k + 1)
                        v.memset(sums[:, :, RING:RING + WIN], 0.0).then_inc(folded, 1)

                    def split(k, u):
                        dve.wait_ge(unit_copied, k * UNITS + u + 1)
                        for i in range(2):
                            n = slice(i * HALF, (i + 1) * HALF)
                            r = v.tensor_tensor(unit_l[:, u % 2, :, n],
                                                sums[:, u * UNIT:(u + 1) * UNIT, bass.ds((k * BLK + i * HALF) % RING, HALF)],
                                                unit_h[:, u % 2, :, n].bitcast(F32), ALU.subtract)
                        r.then_inc(unit_split, 1)

                    def evacuate(k, n):
                        dve.wait_ge(block_done, k + 2)
                        dve.wait_ge(x_in, 16 * k + 16)
                        if not isinstance(k, int) or k >= 1:
                            dve.wait_ge(out_written, 16 * k)
                        v.tensor_tensor(y[0:n, :], out_ps[0:n, :], xres[0:n, :], ALU.add).then_inc(evacuated, 1)

                    def norm(k, n, i):
                        if i == 0:
                            dve.wait_ge(evacuated, k + 2)
                            v.tensor_tensor(y[0:n, :], y[0:n, :], bias_all[0:n, :], ALU.add).then_inc(norm_v, 1)
                        if i == 1:
                            dve.wait_ge(norm_v, 5 * k + 1)
                            v.bn_stats(stats[0:n, :], y[0:n, :]).then_inc(norm_v, 1)
                            dve.wait_ge(norm_v, 5 * k + 2)
                            dve.sem_inc(dve_turns, 1)
                            v.bn_aggr(mv[0:n, :], stats[0:n, :]).then_inc(norm_v, 1)
                        if i == 2:
                            dve.wait_ge(norm_a, 2 * k + 1)
                            v.reciprocal(sd[0:n, 1:2], sd[0:n, 0:1]).then_inc(norm_v, 1)
                            dve.wait_ge(norm_v, 5 * k + 4)
                            v.tensor_scalar(sd[0:n, 2:3], mv[0:n, 0:1], sd[0:n, 1:2], -1.0, ALU.mult, ALU.mult).then_inc(norm_v, 1)

                    def bases_low(i):
                        dve.wait_ge(high_ready, i + 1)
                        v.tensor_tensor(bases_l[:, bass.ds(i, 1), :].rearrange("p o f -> p (o f)"), (y, xres)[i_par[0]][:, :],
                                        bases_h[:, bass.ds(i, 1), :].rearrange("p o f -> p (o f)").bitcast(F32),
                                        ALU.subtract).then_inc(low_ready, 1)
                    i_par = [0]

                    window(0, 0)
                    where = positions(0)
                    for t in range(SLOTS):
                        for i in range(PRE + 2 * t, min(NSB, PRE + 2 * t + 2)):
                            coefs(i)
                        add_part(t, t, where)
                        if t == 1:
                            window(1, 1)
                    dve.wait_ge(coef_ready, NSB)
                    with dve.Fori(0, PAIRS) as h:
                        done = 0
                        for s in range(2 * SLOTS):
                            g = s // SLOTS + 1
                            if s % SLOTS == 0:
                                where = positions(h * (2 * SLOTS) + g * SLOTS)
                            add_part(h * (2 * SLOTS) + (SLOTS + s), s, where)
                            if s % SLOTS == 1:
                                window(h * 2 + (g + 1), (g + 1) % 2)
                            if (s + 1) * SPW // (2 * SLOTS) > done:
                                i_par[0] = done % 2
                                bases_low(h * SPW + done)
                                done += 1

                    def step(k, p, where, last=T):
                        t = k * TPB + (HEAD + p)
                        if not isinstance(t, int) or t < last:
                            g = k * GPB + (HEAD + p) // SLOTS
                            if p % SLOTS == 0:
                                where = positions(t, min(SLOTS, last - t) if isinstance(t, int) else SLOTS)
                            add_part(t, p, where)
                            if p % SLOTS == 1:
                                window(g + 1, ((HEAD + p) // SLOTS + 1) % 2,
                                       min(SLOTS, last - (g + 1) * SLOTS) if isinstance(g, int) else SLOTS)
                        if p % UNIT == 1 and p // UNIT < LOWS:
                            split(k, p // UNIT)
                        return where

                    def opening(k, where):
                        for p in range(SLOTS):
                            where = step(k, p, where)
                            if not (isinstance(k, int) and k == 0) and 2 <= p < 5:
                                norm(k - 1, BLK, p - 2)
                        return where

                    fold(0, HEAD)
                    opening(0, where)
                    with dve.Fori(0, NBLK - 2) as k:
                        for p in range(SLOTS, TPB):
                            where = step(k, p, where)
                        fold(k + 1, k * TPB + (HEAD + TPB))
                        evacuate(k, BLK)
                        opening(k + 1, where)
                    for p in range(SLOTS, TPB):
                        where = step(NBLK - 2, p, where)
                        if TAIL + p == T - 1:
                            closing = p
                    fold(NBLK - 1, T)
                    evacuate(NBLK - 2, BLK)
                    for u in range(LOWS):
                        split(NBLK - 1, u)
                        if u < 3:
                            norm(NBLK - 2, BLK, u)
                    n = N - (NBLK - 1) * BLK
                    evacuate(NBLK - 1, n)
                    for i in range(3):
                        norm(NBLK - 1, n, i)
                with dve.Else():
                    for i in range(PRE, NSB):
                        coefs(i)
                    dve.wait_ge(coef_ready, NSB)
                    dve.wait_ge(tables, 4)
                    gr = slice(0, GEN)
                    dve.sem_inc(g_sum, 1)
                    with dve.Fori(0, N // GEN) as w:
                        with dve.Fori(0, T) as t:
                            dve.wait_ge(g_step, w * T + t + 1)
                            v.scalar_tensor_tensor(
                                gwin, node_iota[:, :].unsqueeze(1).to_broadcast([P, NB, GEN]),
                                dstc[:, bass.ds(t, 1)],
                                coef[:, bass.ds(t, 1), :].rearrange("p o b -> p (o b)").unsqueeze(2).to_broadcast([P, NB, GEN]),
                                ALU.is_equal, ALU.mult).then_inc(g_win, 1)
                        dve.wait_ge(g_mm, w * T + T)
                        for c in range(IC):
                            v.tensor_copy(gsum[:, c * NB:(c + 1) * NB, :], banks[:, c, 0:NB * GEN].rearrange("p (b n) -> p b n", b=NB))
                        v.tensor_scalar(dstc[:, :], dstc[:, :], float(-GEN), None, ALU.add).then_inc(g_sum, 1)
                        dve.wait_ge(g_sum, w + 2)
                        dve.sem_inc(g_out, 1)
                        dve.wait_ge(g_done, w + 1)
                        dve.wait_ge(g_x, 16 * w + 16)
                        v.tensor_tensor(y[gr, :], out_ps[gr, :], xres[gr, :], ALU.add).then_inc(g_v, 1)
                        dve.wait_ge(g_v, 6 * w + 1)
                        v.tensor_tensor(y[gr, :], y[gr, :], bias_all[gr, :], ALU.add).then_inc(g_v, 1)
                        dve.wait_ge(g_v, 6 * w + 2)
                        v.bn_stats(stats[gr, :], y[gr, :]).then_inc(g_v, 1)
                        dve.wait_ge(g_v, 6 * w + 3)
                        dve.sem_inc(dve_turns, 1)
                        v.bn_aggr(mv[gr, :], stats[gr, :]).then_inc(g_v, 1)
                        dve.wait_ge(g_a, 2 * w + 1)
                        v.reciprocal(sd[gr, 1:2], sd[gr, 0:1]).then_inc(g_v, 1)
                        dve.wait_ge(g_v, 6 * w + 5)
                        v.tensor_scalar(sd[gr, 2:3], mv[gr, 0:1], sd[gr, 1:2], -1.0, ALU.mult, ALU.mult).then_inc(g_v, 1)
                        dve.wait_ge(g_w, 16 * w + 16)

            @block.scalar
            def _(act):
                a = nc.scalar
                act.wait_ge(consts, 1)
                a.activation(pick.rearrange("p (t r) -> p t r", r=R), ident[:, :].unsqueeze(2).to_broadcast([P, P, R]),
                             ACT.Copy).then_inc(picked, 1)
                act.wait_ge(swept, 2)
                a.activation(sums[:, POOL_PLANES:PL, :], zero[:, 0:1].unsqueeze(2).to_broadcast([P, PL - POOL_PLANES, RING + WIN]),
                             ACT.Copy).then_inc(swept, 1)

                def types(i):
                    nq = min(SB, QN - i * SB)
                    act.wait_ge(type_done, i + 1)
                    if i >= 2:
                        act.wait_ge(hot_ready, i)
                    a.activation(et_all[:, i % 2, 0:nq, :], type_ps[:, 0:nq * P].rearrange("p (q e) -> p q e", e=P), ACT.Copy).then_inc(type_copied, 1)
                for i in range(PRE + 1):
                    types(i)

                def load_bases():
                    act.wait_ge(coef_done, NSB)
                    for c in range(SPLIT, IC):
                        act.dma_start(bases_f[:, (c - SPLIT) * NB:(c - SPLIT + 1) * NB, :],
                                      bases[:, c * P:(c + 1) * P, :].rearrange("b p o -> p b o")).then_inc(basesf_in[c - SPLIT], 16)
                act.wait_ge(flag_ready, 1)
                ok = act.value_load(flag[0:1, 0:1], min_val=0, max_val=1)
                with act.If(ok == 1):
                    act.sem_inc(unit_free, 1)
                    act.sem_inc(block_done, 1)
                    act.sem_inc(evacuated, 1)
                    act.sem_inc(part_added, 1)
                    stage = (y, xres)

                    def load_raw(i, b):
                        p = bases[i % NB, bass.ds(i // NB * P, P), :] if isinstance(i, int) else None
                        act.dma_start(stage[b][:, :], p).then_inc(raw_in[b], 16)

                    def high(i, b, wait):
                        act.wait_ge(raw_in[b], wait)
                        act.sem_inc(act_turns, 1)
                        a.activation(bases_h[:, i, :], stage[b][:, :], ACT.Copy).then_inc(high_ready, 1)
                    load_raw(0, 0)
                    load_raw(1, 1)
                    for i in range(PRE + 1, NSB):
                        types(i)
                    load_bases()
                    for i in range(SPLIT * NB):
                        high(i, i % 2, 16 * (i // 2) + 16)
                        if i >= 1 and i + 1 < SPLIT * NB:
                            act.wait_ge(low_ready, i)
                            load_raw(i + 1, (i + 1) % 2)

                    def unit(k, u):
                        if u == 0:
                            act.wait_ge(folded, 2 * k + 2)
                            act.wait_ge(unit_free, k * (UNITS - 1) + 1)
                        elif u == 1:
                            act.wait_ge(block_done, k + 1)
                        else:
                            act.wait_ge(unit_free, k * (UNITS - 1) + u)
                        act.sem_inc(act_turns, 1)
                        to = unit_h if u < LOWS else unit_f
                        planes = [sums[:, u * UNIT:(u + 1) * UNIT, bass.ds((k * BLK + i * HALF) % RING, HALF)] for i in range(2)]
                        for i in range(2):
                            r = a.activation(to[:, u % 2, :, i * HALF:(i + 1) * HALF], planes[i], ACT.Copy)
                        r.then_inc(unit_copied, 1)
                        if u < LOWS:
                            act.wait_ge(unit_split, k * LOWS + u + 1)
                        else:
                            act.wait_ge(unit_copied, k * UNITS + u + 1)
                        act.sem_inc(act_turns, 1)
                        for i in range(2):
                            r = a.activation(planes[i], zero[:, 0:1].unsqueeze(2).to_broadcast([P, UNIT, HALF]), ACT.Copy)
                        r.then_inc(cleaned, 1)

                    def load_x(k, rows_x, n):
                        act.wait_ge(evacuated, k + 1)
                        act.dma_start(xres[0:n, :], rows_x).then_inc(x_in, 16)

                    def deviation(k, n):
                        act.wait_ge(norm_v, 5 * k + 3)
                        a.activation(sd[0:n, 0:1], mv[0:n, 1:2], ACT.Sqrt, bias=eps[0:n, 0:1]).then_inc(norm_a, 1)

                    def finish(k, n, out_k):
                        act.wait_ge(norm_v, 5 * k + 5)
                        a.activation(y[0:n, :], y[0:n, :], ACT.Identity, bias=sd[0:n, 2:3],
                                     scale=sd[0:n, 1:2]).then_inc(norm_a, 1)
                        act.wait_ge(norm_a, 2 * k + 2)
                        act.dma_start(out_k, y[0:n, :]).then_inc(out_written, 16)

                    act.wait_ge(low_ready, SPLIT * NB)
                    load_x(0, x[0:BLK, :], BLK)
                    unit(0, 0)
                    unit(0, 1)
                    with act.Fori(0, NBLK - 2) as k:
                        for u in range(2, UNITS):
                            unit(k, u)
                        load_x(k + 1, x[bass.ds(k * BLK + BLK, BLK), :], BLK)
                        unit(k + 1, 0)
                        deviation(k, BLK)
                        unit(k + 1, 1)
                        finish(k, BLK, out[bass.ds(k * BLK, BLK), :])
                    k = NBLK - 2
                    n = N - (NBLK - 1) * BLK
                    for u in range(2, UNITS):
                        unit(k, u)
                    load_x(k + 1, x[k * BLK + BLK:N, :], n)
                    unit(k + 1, 0)
                    unit(k + 1, 1)
                    deviation(k, BLK)
                    unit(k + 1, 2)
                    finish(k, BLK, out[k * BLK:k * BLK + BLK, :])
                    for u in range(3, UNITS):
                        unit(k + 1, u)
                    deviation(k + 1, n)
                    finish(k + 1, n, out[k * BLK + BLK:N, :])
                    act.wait_ge(out_written, 16 * NBLK)
                with act.Else():
                    for i in range(PRE + 1, NSB):
                        types(i)
                    load_bases()
                    gr = slice(0, GEN)
                    for s in range(SLOTS):
                        act.wait_ge(row_in[s], 16)
                    for p in range(4):
                        act.sem_inc(g_used, 1)
                    with act.Fori(0, N // GEN) as w:
                        act.dma_start(xres[gr, :], x[bass.ds(w * GEN, GEN), :]).then_inc(g_x, 16)

                        def step(i, t, b):
                            a.copy(gidx[:, b:b + 1], idx[:, bass.ds(t, 1)]).then_inc(g_idx, 1)
                            act.sem_inc(g_step, 1)
                            act.wait_ge(g_mm, i + 1)
                        with act.Fori(0, T // 2) as h:
                            step(w * T + 2 * h, 2 * h, 0)
                            step(w * T + 2 * h + 1, 2 * h + 1, 1)
                        step(w * T + T - 1, T - 1, 0)
                        act.wait_ge(g_v, 6 * w + 4)
                        a.activation(sd[gr, 0:1], mv[gr, 1:2], ACT.Sqrt, bias=eps[gr, 0:1]).then_inc(g_a, 1)
                        act.wait_ge(g_v, 6 * w + 6)
                        a.activation(y[gr, :], y[gr, :], ACT.Identity, bias=sd[gr, 2:3], scale=sd[gr, 1:2]).then_inc(g_a, 1)
                        act.wait_ge(g_a, 2 * w + 2)
                        act.dma_start(out[bass.ds(w * GEN, GEN), :], y[gr, :]).then_inc(g_w, 16)
                        act.wait_ge(g_w, 16 * w + 16)


_INS = ["x", "src", "dst", "edge_type_32", "edge_weight1", "L0_gnn_bases", "L0_gnn_w_comp", "L0_gnn_h_bias"]


def kernel(**inputs):
    import numpy as np
    import concourse.bacc as bacc
    from concourse import mybir
    from concourse.bass_utils import run_bass_kernel_spmd

    nc = bacc.Bacc("TRN2", target_bir_lowering=False, num_devices=1)
    arrays, args = {}, []
    for name in _INS:
        a = np.ascontiguousarray(inputs[name])
        arrays[f"in_{name}"] = a
        args.append(nc.dram_tensor(f"in_{name}", a.shape, mybir.dt.from_np(a.dtype), kind="ExternalInput").ap())
    args.append(nc.dram_tensor("out", inputs["x"].shape, mybir.dt.float32, kind="ExternalOutput").ap())
    rgcn_resnorm(nc, *args)
    r = run_bass_kernel_spmd(nc, [arrays], core_ids=[0])
    return r.results[0]["out"]
```

```python
from contextlib import ExitStack

import concourse.bass as bass
from concourse import mybir

ALU = mybir.AluOpType
ACT = mybir.ActivationFunctionType
AX_X = mybir.AxisListType.X
F32 = mybir.dt.float32
I32 = mybir.dt.int32
U32 = mybir.dt.uint32
BF16 = mybir.dt.bfloat16
F32R = mybir.dt.float32r

P = 128
EPS = 1e-5
WIN = 8
BLK = P
HALF = BLK // 2
RING = 5 * HALF
SLOTS = 8
LATE = 8
EARLY = 8
PARTS = 4
UNIT = 4
WARM_TILES = 6
LAG = 4
SPLIT = 28
GEN = 50
POOL_PLANES = 16


def rgcn_resnorm(nc, x, src, dst, etype, weight, bases, w_comp, h_bias, out):
    N, F = x.shape
    E = src.shape[0]
    R, NB = w_comp.shape
    T = -(-E // P)
    LAST = E - (T - 1) * P
    TC = -(-T // P)
    IC = F // P
    PL = IC * NB
    NBLK = -(-N // BLK)
    TPB = E * BLK // (N * P)
    NPT = BLK // TPB
    UNITS = PL // UNIT
    RAWS = 2
    AHEAD = 4
    LOWS_FIRST = 10
    LOWS = SPLIT // UNIT
    HEAD = TPB + LATE
    GPB = TPB // SLOTS
    NG = -(-T // SLOTS)
    TG = NG * SLOTS
    TAIL = HEAD + (NBLK - 2) * TPB
    Q = P // R
    SB = 4
    BT = SB * Q
    QN = -(-T // Q)
    NSB = -(-QN // SB)
    PICKED = P * R // (2 * F)
    PRE = 1
    assert E * BLK == TPB * N * P and LAST * 2 == P and NG % 2 == 0 and T == (NG - 1) * SLOTS + 1
    assert HEAD % SLOTS == 0 and PL == TPB and N % GEN == 0
    assert 2 * (NSB - 1) <= HEAD and SPLIT % UNIT == 0 and PICKED <= PL - SPLIT and NB % RAWS == 0
    assert NPT * (TPB * 2 - 1 + HEAD - TPB + EARLY) - RING < BLK + NPT * LATE

    with ExitStack() as ctx:
        def sb(name, shape, dt=F32, stack=ctx):
            return stack.enter_context(nc.sbuf_tensor(name, shape, dt))

        def psum(name, shape):
            return ctx.enter_context(nc.psum_tensor(name, shape, F32))

        def sem(name):
            return ctx.enter_context(nc.semaphore(name))

        rows = sb("rows", [P, SLOTS, F])
        sums = sb("sums", [P, PL, RING + WIN])
        hot8 = sb("hot8", [P, 2, SLOTS, WIN])
        win = sb("win", [P, 2, SLOTS, NB, WIN])
        unit_f = sb("unit_f", [P, UNITS - LOWS, UNIT, BLK])
        y = sb("y", [P, F])
        stats = sb("stats", [P, 6])
        mv = sb("mv", [P, 2])
        sd = sb("sd", [P, 4])
        bases_f = sb("bases_f", [P, PL - SPLIT, F])
        with ExitStack() as before:
            et_all = sb("et_all", [P, 2, SB, P], BF16, before)
            et_hot = sb("et_hot", [P, 2, SB, P], BF16, before)
            wgt = sb("wgt", [P, TG], F32, before)
            et_b = sb("et_b", [P, TC, P], BF16, before)
            w_diag = sb("w_diag", [P, Q * NB], F32, before)
            w_rest = sb("w_rest", [P, 2, Q * NB], F32, before)
            tile_nodes = sb("tile_nodes", [P, TC], F32, before)
            base = sb("base", [P, TC], F32, before)
            top = sb("top", [P, TC], F32, before)
            chk = sb("chk", [P, 4, TC], F32, before)
            bad = sb("bad", [P, 1], F32, before)
            pos = sb("pos", [P, 4, TC], F32, before)
            idx = sb("idx", [P, TG], U32, before)
            rel_f = sb("rel_f", [P, TC, P], F32, before)
            wgt_t = sb("wgt_t", [P, TC, P], F32, before)
            dst_f = sb("dst_f", [P, TC, P], F32, before)
            src_i = sb("src_i", [P, TC, P], I32, before)
            et_i = sb("et_i", [P, TC, P], I32, before)
            ident = sb("ident", [P, P], F32, before)
        unit_h = sb("unit_h", [P, 2, UNIT, BLK], F32R)
        unit_l = sb("unit_l", [P, 2, UNIT, BLK], F32R)
        bases_h = sb("bases_h", [P, SPLIT, F], F32R)
        with ExitStack() as before:
            raw = sb("raw", [P, SPLIT, F], F32, before)
        bases_l = sb("bases_l", [P, SPLIT, F], F32R)
        idx_table = nc.dram_tensor("idx_table", [P, TG], U32).ap()
        rel = sb("rel", [P, TG], BF16)
        coef = sb("coef", [P, QN * Q, NB])
        idx_s = sb("idx_s", [P, 2, SLOTS], U32)
        pos_row = sb("pos_row", [1, TG], I32)
        flag = sb("flag", [1, 1], I32)
        ones = sb("ones", [P, 1])
        zero = sb("zero", [P, 1])
        eps = sb("eps", [P, 1])
        node_iota = sb("node_iota", [P, GEN])
        part_no = sb("part_no", [P, 1])
        rel_of_part = sb("rel_of_part", [P, Q])
        with ExitStack() as before:
            w_part = sb("w_part", [P, 3, Q * NB], BF16, before)
        bias_all = sb("bias_all", [P, F])
        flat_win = [win[:, g, :, :, :].rearrange("p t b n -> p (t b n)") for g in range(2)]
        flat_unit = unit_f[:, :, :, :].rearrange("p g j n -> p (g j n)")

        def early(flat, at=0):
            return flat[:, at:at + TC * P].rearrange("p (c e) -> p c e", e=P)
        src_f = early(flat_win[0])
        pick = bases_f[:, PL - SPLIT - PICKED:, :].rearrange("p b f -> p (b f)").bitcast(BF16)
        dst_i = early(flat_win[1]).bitcast(I32)
        dstc = flat_unit[:, 0:TG]
        gidx = idx_s[:, 0, 0:2]
        gwin = win[:, :, :, :, :].rearrange("p g t b n -> p (g t b n)")[:, 0:NB * GEN].rearrange("p (b n) -> p b n", b=NB)
        gsum = sums[:, :, 0:GEN]
        banks = psum("banks", [P, 8, 512])
        part = banks[:, 0:PARTS, 0:PL * WIN]
        type_ps = banks[:, 4, :]
        coef_bank = banks[:, 5, :]
        out_ps = banks[:, 6, :]
        small_ps = banks[:, 7, :]

        src_in, dst_in, et_in, wgt_in = sem("src_in"), sem("dst_in"), sem("et_in"), sem("wgt_in")
        const_in, bias_in = sem("const_in"), sem("bias_in")
        basesf_in = sem("basesf_in")
        raw_in = [sem(f"raw_in{i}") for i in range(SPLIT // RAWS)]
        high_ready, low_ready = sem("high_ready"), sem("low_ready")
        consts, pool_c, swept = sem("consts"), sem("pool_c"), sem("swept")
        cleared, prep, chained, picked = sem("cleared"), sem("prep"), sem("chained"), sem("picked")
        transposed, tables = sem("transposed"), sem("tables")
        type_done, type_copied, hot_ready, coef_done, coef_ready = (
            sem("type_done"), sem("type_copied"), sem("hot_ready"), sem("coef_done"), sem("coef_ready"))
        row_in = [sem(f"row_in{s}") for s in range(SLOTS)]
        idx_out, idx_in = sem("idx_out"), [sem("idx_in0"), sem("idx_in1")]
        flag_ready = sem("flag_ready")
        turns, dve_turns, act_turns = sem("turns"), sem("dve_turns"), sem("act_turns")
        hot8_ready, win_ready, part_ready, part_added = (
            sem("hot8_ready"), sem("win_ready"), sem("part_ready"), sem("part_added"))
        folded, unit_copied, unit_split, unit_free = sem("folded"), sem("unit_copied"), sem("unit_split"), sem("unit_free")
        cleaned = sem("cleaned")
        block_done, evacuated = sem("block_done"), sem("evacuated")
        x_in, out_written = sem("x_in"), sem("out_written")
        norm_v, norm_a = sem("norm_v"), sem("norm_a")
        g_step, g_idx, g_win, g_mm = sem("g_step"), sem("g_idx"), sem("g_win"), sem("g_mm")
        g_row = [sem("g_row0"), sem("g_row1")]
        g_base = [sem(f"g_base{i}") for i in range(4)]
        g_used, g_done = sem("g_used"), sem("g_done")
        g_sum, g_out, g_v, g_a, g_x, g_w = sem("g_sum"), sem("g_out"), sem("g_v"), sem("g_a"), sem("g_x"), sem("g_w")

        TL = T - (TC - 1) * P
        full = (TC - 1) * P * P

        def high_at(t):
            def until(t):
                return min(SPLIT, t * SPLIT // (HEAD - 4))
            return range(until(t), until(t + 1))

        def low_at(t):
            def until(t):
                if t <= HEAD:
                    return min(LOWS_FIRST, t * LOWS_FIRST // (HEAD - 4))
                return min(SPLIT, LOWS_FIRST + (t - HEAD) * 2 // 3)
            return range(until(t), until(t + 1))

        def load_whole(eng, i, n):
            p = SPLIT + i
            eng.dma_start(bases_f[:, i:i + n, :],
                          bases[p % NB:p % NB + n, p // NB * P:(p // NB + 1) * P, :].rearrange("b p o -> p b o")).then_inc(basesf_in, 16)

        with nc.Block() as block:

            @block.sync
            def _(sp):
                for n, (a, t, s) in enumerate(((src, src_i, src_in), (dst, dst_i, dst_in), (etype, et_i, et_in),
                                               (weight.rearrange("e o -> (e o)"), wgt_t, wgt_in))):
                    if n == 3:
                        sp.wait_ge(cleared, 5)
                        for j in range(Q):
                            sp.dma_start(w_diag[R * j:R * j + R, NB * j:NB * j + NB], w_comp).then_inc(const_in, 16)
                    sp.dma_start(t[:, 0:TC - 1, :], a[0:full].rearrange("(c p e) -> p c e", p=P, e=P)).then_inc(s, 16)
                    sp.wait_ge(cleared, n + 1)
                    sp.dma_start(t[0:TL - 1, TC - 1, :], a[full:full + (TL - 1) * P].rearrange("(p e) -> p e", e=P)).then_inc(s, 16)
                    half = a[E - LAST:E].unsqueeze(0)
                    sp.dma_start(t[TL - 1:TL, TC - 1, 0:LAST], half).then_inc(s, 16)
                    if n < 3:
                        sp.dma_start(t[TL - 1:TL, TC - 1, LAST:P], half).then_inc(s, 16)
                sp.wait_ge(tables, 1)
                sp.dma_start(idx_table, idx[:, :]).then_inc(idx_out, 16)
                sp.wait_ge(idx_out, 16)
                sp.wait_ge(flag_ready, 1)
                ok = sp.value_load(flag[0:1, 0:1], min_val=0, max_val=1)
                with sp.If(ok == 1):
                    def stage(g, par, wait):
                        if wait is not None:
                            sp.wait_ge(row_in[SLOTS - 1], wait)
                        sp.dma_start(idx_s[:, par, :], idx_table[:, bass.ds(g * SLOTS, SLOTS)]).then_inc(idx_in[par], 16)

                    def load_raw(i):
                        sp.dma_start(raw[:, i:i + RAWS, :], bases[i % NB:i % NB + RAWS, i // NB * P:(i // NB + 1) * P, :]
                                     .rearrange("b p o -> p b o")).then_inc(raw_in[i // RAWS], 16)
                    for t in range(-AHEAD, HEAD + TPB - 1):
                        if t == 0:
                            stage(1, 1, None)
                        if t >= SLOTS - 1 and t % SLOTS == SLOTS - 1:
                            g = t // SLOTS + 2
                            stage(g, g % 2, 16 * g - 16)
                        for i in high_at(t + AHEAD):
                            if i % RAWS == 0:
                                if t >= 0:
                                    sp.wait_ge(row_in[t % SLOTS], 16 * (t // SLOTS) + 16)
                                load_raw(i)
                        if t >= HEAD and t % 4 == 3 and (t - HEAD) // 4 < (PL - SPLIT) // RAWS:
                            sp.wait_ge(type_done, NSB)
                            sp.wait_ge(row_in[t % SLOTS], 16 * (t // SLOTS) + 16)
                            load_whole(sp, (t - HEAD) // 4 * RAWS, RAWS)
                    with sp.Fori((HEAD + TPB) // SLOTS // 2 + 1, NG // 2) as h:
                        stage(2 * h, 0, 32 * h - 16)
                        stage(2 * h + 1, 1, 32 * h)
                with sp.Else():
                    with sp.Fori(0, N // GEN) as w:
                        for p in range(SPLIT):
                            sp.wait_ge(g_used, w * SPLIT + p + 1)
                            sp.dma_start(rows[:, 4 + p % 4, :], bases[p % NB, p // NB * P:(p // NB + 1) * P, :]).then_inc(g_base[p % 4], 16)

            @block.gpsimd
            def _(pool):
                nc.gpsimd.memset(ident[:, :], 0.0).then_inc(pool_c, 1)
                pool.wait_ge(pool_c, 1)
                nc.gpsimd.affine_select(out=ident[:, :], in_=ident[:, :], compare_op=ALU.not_equal, fill=1.0,
                                        base=0, pattern=[[-1, P]], channel_multiplier=1).then_inc(consts, 1)
                nc.gpsimd.iota(node_iota[:, :], [[1, GEN]], base=0, channel_multiplier=0,
                               allow_small_or_imprecise_dtypes=True).then_inc(consts, 1)
                nc.gpsimd.iota(tile_nodes[:, :], [[NPT * P, TC]], base=0, channel_multiplier=NPT,
                               allow_small_or_imprecise_dtypes=True).then_inc(consts, 1)
                nc.gpsimd.iota(part_no[:, :], [[1, 1]], base=0, channel_multiplier=1,
                               allow_small_or_imprecise_dtypes=True).then_inc(consts, 1)
                nc.gpsimd.memset(sums[:, 0:POOL_PLANES, :], 0.0).then_inc(swept, 1)

                def gather(s, index):
                    return pool.indirect_dma_start(rows[:, s, :], None, x, bass.IndirectOffsetOnAxis(index, 0))

                pool.wait_ge(tables, 1)
                for s in range(SLOTS):
                    gather(s, idx[:, s:s + 1]).then_inc(row_in[s], 16)
                pool.wait_ge(flag_ready, 1)
                ok = pool.value_load(flag[0:1, 0:1], min_val=0, max_val=1)
                with pool.If(ok == 1):
                    def group(par, idx_wait, first_tile, slots=SLOTS):
                        pool.wait_ge(idx_in[par], idx_wait)
                        pool.sem_inc(turns, 1)
                        for s in range(slots):
                            pool.wait_ge(part_ready, first_tile + s - SLOTS + 1)
                            pool.sem_inc(turns, 1)
                            gather(s, idx_s[:, par, s:s + 1]).then_inc(row_in[s], 16)
                    group(1, 16, SLOTS)
                    with pool.Fori(1, NG // 2 - 1) as h:
                        group(0, 16 * h, 2 * SLOTS * h)
                        group(1, 16 * h + 16, 2 * SLOTS * h + SLOTS)
                    h = NG // 2 - 1
                    group(0, 16 * h, 2 * SLOTS * h)
                    group(1, 16 * h + 16, 2 * SLOTS * h + SLOTS, 1)
                with pool.Else():
                    for s in range(SLOTS):
                        pool.wait_ge(row_in[s], 16)

                    def general(i, b):
                        pool.wait_ge(g_idx, i + 1)
                        pool.sem_inc(turns, 1)
                        gather(b, gidx[:, b:b + 1]).then_inc(g_row[b], 16)
                    with pool.Fori(0, N // GEN) as w:
                        with pool.Fori(0, T // 2) as h:
                            general(w * T + 2 * h, 0)
                            general(w * T + 2 * h + 1, 1)
                        general(w * T + T - 1, 0)

            @block.tensor
            def _(pe):
                pe.wait_ge(consts, 1)

                def table(n, a, s, v):
                    pe.wait_ge(s, v)
                    for c in range(TC):
                        m = nc.tensor.transpose(banks[:, n, c * P:(c + 1) * P], a[:, c, :], ident[:, :])
                    m.then_inc(transposed, 1)

                def types(i):
                    pe.wait_ge(picked, 1)
                    pe.wait_ge(hot_ready, 1)
                    if i >= 1:
                        pe.wait_ge(type_copied, i)
                    for q in range(i * SB, min(QN, i * SB + SB)):
                        c, t = q * Q // P, q * Q % P
                        m = nc.tensor.matmul(type_ps[:, (q - i * SB) * P:(q - i * SB + 1) * P],
                                             pick[:, t * R:(t + Q) * R], et_b[:, c, :],
                                             start=True, stop=True)
                    m.then_inc(type_done, 1)

                def coefs(i):
                    if i + 1 < NSB:
                        types(i + 1)
                    pe.wait_ge(hot_ready, i + 2)
                    if i >= 1:
                        pe.wait_ge(coef_ready, i)
                    nq = min(SB, QN - i * SB)
                    for q in range(nq):
                        for w in range(3):
                            m = nc.tensor.matmul(coef_bank[:, q * Q * NB:(q + 1) * Q * NB], et_hot[:, i % 2, q, :],
                                                 w_part[:, w, :], start=(w == 0), stop=(w == 2))
                    m.then_inc(coef_done, 1)

                def keep_warm(bank):
                    nc.tensor.matmul(bank[:, 0:TC * P], et_b[:, 0, :], et_b[:, :, :].rearrange("p c e -> p (c e)"), start=True, stop=True)

                table(0, src_f, prep, 1)
                table(1, rel_f, prep, 2)
                types(0)
                pe.wait_ge(prep, 3)
                for c in range(TC):
                    nc.tensor.transpose(small_ps[0:1, c * P:(c + 1) * P], pos[:, 3, c:c + 1], ident[:, :])
                nc.tensor.matmul(out_ps[0:1, 0:1], bad[:, 0:1], ones[:, 0:1], start=True, stop=True).then_inc(transposed, 1)
                table(2, wgt_t, wgt_in, 48)
                for i in range(PRE):
                    coefs(i)
                pe.wait_ge(tables, 3)
                pe.wait_ge(flag_ready, 1)
                ok = pe.value_load(flag[0:1, 0:1], min_val=0, max_val=1)
                with pe.If(ok == 1):
                    def tile_product(t, s, par, row_wait, win_wait):
                        pe.wait_ge(row_in[s], row_wait)
                        if s == 0:
                            pe.wait_ge(win_ready, win_wait)
                        pe.wait_ge(part_added, t - PARTS + 2 if not isinstance(t, int) or t >= PARTS else 1)
                        for c in range(IC):
                            m = nc.tensor.matmul(part[:, s % PARTS, c * NB * WIN:(c + 1) * NB * WIN],
                                                 rows[:, s, c * P:(c + 1) * P], win[:, par, s, :, :],
                                                 start=True, stop=True)
                        m.then_inc(part_ready, 1)

                    def plane_product(k, p):
                        u, j, b = p // UNIT, p % UNIT, p // UNIT % 2
                        if p == 0:
                            pe.wait_ge(evacuated, k + 1)
                        first, last = p == 0, p == PL - 1
                        if p < SPLIT:
                            if j == 0:
                                pe.wait_ge(low_ready, p + UNIT)
                                pe.wait_ge(unit_split, k * LOWS + u + 1)
                            nc.tensor.matmul(out_ps, unit_h[:, b, j, :], bases_h[:, p, :], start=first, stop=False)
                            nc.tensor.matmul(out_ps, unit_l[:, b, j, :], bases_h[:, p, :], start=False, stop=False)
                            m = nc.tensor.matmul(out_ps, unit_h[:, b, j, :], bases_l[:, p, :], start=False, stop=last)
                        else:
                            if p == SPLIT:
                                pe.wait_ge(basesf_in, 16 * (PL - SPLIT) // RAWS)
                            if j == 0:
                                pe.wait_ge(unit_copied, k * UNITS + u + 1)
                            m = nc.tensor.matmul(out_ps, unit_f[:, u - LOWS, j, :], bases_f[:, p - SPLIT, :], start=first, stop=last)
                        if last:
                            m.then_inc(block_done, 1)
                        elif j == UNIT - 1:
                            m.then_inc(unit_free, 1)

                    for t in range(HEAD):
                        g = t // SLOTS
                        tile_product(t, t % SLOTS, g % 2, g * 16 + 16, g + 1)
                        if t % 2 == 0 and t // 2 + PRE < NSB:
                            coefs(t // 2 + PRE)
                        for _ in range(2 if t < WARM_TILES else t % 2 if t < HEAD - 1 else 0):
                            keep_warm(out_ps)
                    with pe.Fori(0, NBLK - 2) as k:
                        for p in range(PL):
                            g = (HEAD + p) // SLOTS
                            tile_product(k * TPB + (HEAD + p), p % SLOTS, g % 2, k * (GPB * 16) + (g * 16 + 16), k * GPB + (g + 1))
                            if p >= LAG:
                                plane_product(k, p - LAG)
                        for p in range(PL - LAG, PL):
                            plane_product(k, p)
                    for p in range(PL + LAG):
                        t = TAIL + p
                        if t < T:
                            g = t // SLOTS
                            tile_product(t, t % SLOTS, g % 2, g * 16 + 16, g + 1)
                        if p >= LAG:
                            plane_product(NBLK - 2, p - LAG)
                    for p in range(PL):
                        plane_product(NBLK - 1, p)
                with pe.Else():
                    table(3, dst_f, prep, 3)
                    for i in range(PRE, NSB):
                        coefs(i)
                    pe.wait_ge(basesf_in, 16 * (PL - SPLIT) // RAWS)
                    with pe.Fori(0, N // GEN) as w:
                        def product(i, b, row_wait, first):
                            pe.wait_ge(g_row[b], row_wait)
                            pe.wait_ge(g_win, i + 1)
                            for c in range(IC):
                                m = nc.tensor.matmul(banks[:, c, 0:NB * GEN], rows[:, b, c * P:(c + 1) * P],
                                                     gwin[:, :, :], start=first, stop=False, skip_group_check=True)
                            m.then_inc(g_mm, 1)
                        pe.wait_ge(g_sum, w + 1)
                        product(w * T, 0, 16 * (T // 2 + 1) * w + 16, True)
                        product(w * T + 1, 1, 16 * (T // 2) * w + 16, False)
                        with pe.Fori(1, T // 2) as h:
                            product(w * T + 2 * h, 0, 16 * (T // 2 + 1) * w + 16 * h + 16, False)
                            product(w * T + 2 * h + 1, 1, 16 * (T // 2) * w + 16 * h + 16, False)
                        product(w * T + T - 1, 0, 16 * (T // 2 + 1) * w + 16 * (T // 2 + 1), False)
                        pe.wait_ge(g_sum, w + 2)
                        pe.wait_ge(g_out, w + 1)
                        for p in range(PL):
                            if p < SPLIT:
                                pe.wait_ge(g_base[p % 4], 16 * (SPLIT // 4) * w + 16 * (p // 4) + 16)
                                right = rows[:, 4 + p % 4, :]
                            else:
                                right = bases_f[:, p - SPLIT, :]
                            m = nc.tensor.matmul(out_ps[0:GEN, :], gsum[:, p, :], right, start=(p == 0), stop=(p == PL - 1))
                            if p < SPLIT:
                                m.then_inc(g_used, 1)
                        m.then_inc(g_done, 1)

            @block.vector
            def _(dve):
                v = nc.vector
                n_chain = [0]

                def chain(ins):
                    n_chain[0] += 1
                    ins.then_inc(chained, 1)
                    dve.wait_ge(chained, n_chain[0])

                v.memset(zero[:, :], 0.0).then_inc(swept, 1)
                for a in (src_i, dst_i, et_i):
                    v.memset(a[:, TC - 1, :], 0).then_inc(cleared, 1)
                v.memset(wgt_t[:, TC - 1, :], 0.0).then_inc(cleared, 1)
                v.memset(w_diag[:, :], 0.0).then_inc(cleared, 1)
                v.memset(ones[:, :], 1.0)
                v.memset(eps[:, :], EPS)
                dve.wait_ge(src_in, 64)
                v.tensor_copy(src_f, src_i[:, :, :]).then_inc(prep, 1)
                dve.wait_ge(consts, 4)
                for j in range(1, Q):
                    r = v.tensor_scalar(rel_of_part[:, j:j + 1], part_no[:, :], float(R * j), float(-R), ALU.is_ge, ALU.mult)
                chain(r)
                dve.wait_ge(transposed, 1)
                v.tensor_copy(idx[:, :], banks[:, 0, 0:TG]).then_inc(tables, 1)
                chain(v.tensor_tensor(rel_of_part[:, 0:1], part_no[:, :], rel_of_part[:, 1:2], ALU.add))
                for j in range(2, Q):
                    chain(v.tensor_tensor(rel_of_part[:, 0:1], rel_of_part[:, 0:1], rel_of_part[:, j:j + 1], ALU.add))
                dve.wait_ge(dst_in, 64)
                chain(v.tensor_copy(dst_f[:, :, :], dst_i[:, :, :]))
                v.tensor_reduce(base[:, :], dst_f[:, :, :], AX_X, ALU.min)
                chain(v.tensor_reduce(top[:, :], dst_f[:, :, :], AX_X, ALU.max))
                v.tensor_tensor(rel_f[:, :, :], dst_f[:, :, :], base[:, :].unsqueeze(2).to_broadcast([P, TC, P]),
                                ALU.subtract).then_inc(prep, 1)
                dve.wait_ge(et_in, 64)
                v.tensor_copy(et_b[:, :, :], et_i[:, :, :]).then_inc(hot_ready, 1)
                v.tensor_tensor(chk[:, 0, :], top[:, :], base[:, :], ALU.subtract)
                v.tensor_tensor(chk[:, 1, :], tile_nodes[:, :], base[:, :], ALU.subtract)
                chain(v.tensor_tensor(chk[:, 2, :], top[:, :], tile_nodes[:, :], ALU.subtract))
                v.tensor_scalar(chk[:, 0, :], chk[:, 0, :], float(WIN), None, ALU.is_ge)
                v.tensor_scalar(chk[:, 1, :], chk[:, 1, :], float(NPT * LATE), None, ALU.is_gt)
                v.tensor_scalar(chk[:, 2, :], chk[:, 2, :], float(NPT * EARLY), None, ALU.is_gt)
                for m in range(1, 4):
                    r = v.tensor_scalar(pos[:, m - 1, :], base[:, :], float(m * RING), float(-RING), ALU.is_ge, ALU.mult)
                chain(r)
                v.tensor_tensor(chk[:, 0, :], chk[:, 0, :], chk[:, 1, :], ALU.add)
                v.tensor_tensor(pos[:, 0, :], pos[:, 0, :], pos[:, 1, :], ALU.add)
                chain(v.tensor_tensor(pos[:, 2, :], pos[:, 2, :], base[:, :], ALU.add))
                v.tensor_tensor(pos[:, 3, :], pos[:, 0, :], pos[:, 2, :], ALU.add)
                chain(v.tensor_tensor(chk[:, 3, :], chk[:, 0, :], chk[:, 2, :], ALU.add))
                chain(v.tensor_reduce(bad[:, :], chk[:, 3, 0:TC - 1], AX_X, ALU.add))
                v.tensor_tensor(bad[0:TL, :], bad[0:TL, :], chk[0:TL, 3, TC - 1:TC], ALU.add).then_inc(prep, 1)
                dve.wait_ge(const_in, 16 * Q)
                chain(v.tensor_copy(w_part[:, 0, :], w_diag[:, :]))
                chain(v.tensor_tensor(w_rest[:, 0, :], w_diag[:, :], w_part[:, 0, :], ALU.subtract))
                chain(v.tensor_copy(w_part[:, 1, :], w_rest[:, 0, :]))
                chain(v.tensor_tensor(w_rest[:, 1, :], w_rest[:, 0, :], w_part[:, 1, :], ALU.subtract))
                chain(v.tensor_copy(w_part[:, 2, :], w_rest[:, 1, :]))
                dve.wait_ge(transposed, 2)
                v.tensor_copy(rel[:, :], banks[:, 1, 0:TG]).then_inc(tables, 1)
                dve.wait_ge(transposed, 3)
                v.tensor_copy(pos_row[:, :], small_ps[0:1, 0:TG]).then_inc(chained, 1)
                n_chain[0] += 1
                v.tensor_scalar(flag[:, :], out_ps[0:1, 0:1], 0.0, None, ALU.is_equal).then_inc(flag_ready, 1)

                def hot(i):
                    nq = min(SB, QN - i * SB)
                    dve.wait_ge(type_copied, i + 1)
                    if i >= 2:
                        dve.wait_ge(coef_done, i - 1)
                    v.tensor_scalar(et_hot[:, i % 2, 0:nq, :], et_all[:, i % 2, 0:nq, :],
                                    rel_of_part[:, 0:1], None, ALU.is_equal).then_inc(hot_ready, 1)

                def coefs(i):
                    nt = min(BT, QN * Q - i * BT)
                    dve.wait_ge(coef_done, i + 1)
                    v.tensor_tensor(coef[:, i * BT:i * BT + nt, :], coef_bank[:, 0:nt * NB].rearrange("p (t b) -> p t b", b=NB),
                                    wgt[:, i * BT:i * BT + nt].unsqueeze(2).to_broadcast([P, nt, NB]), ALU.mult).then_inc(coef_ready, 1)
                hot(0)
                dve.wait_ge(transposed, 4)
                v.tensor_copy(wgt[:, :], banks[:, 2, 0:TG]).then_inc(tables, 1)
                dve.wait_ge(tables, 3)
                for i in range(PRE):
                    hot(i + 1)
                    coefs(i)
                dve.wait_ge(coef_ready, PRE)
                dve.wait_ge(swept, 3)

                def window(g, par, n=SLOTS):
                    if not isinstance(g, int) or g >= 2:
                        dve.wait_ge(part_ready, g * SLOTS - SLOTS)
                    v.tensor_tensor(hot8[:, par, 0:n, :], rel[:, bass.ds(g * SLOTS, n)].unsqueeze(2).to_broadcast([P, n, WIN]),
                                    node_iota[:, 0:WIN].unsqueeze(1).to_broadcast([P, n, WIN]), ALU.is_equal).then_inc(hot8_ready, 1)
                    dve.wait_ge(hot8_ready, g + 1)
                    v.tensor_tensor(win[:, par, 0:n, :, :],
                                    coef[:, bass.ds(g * SLOTS, n), :].unsqueeze(3).to_broadcast([P, n, NB, WIN]),
                                    hot8[:, par, 0:n, :].unsqueeze(2).to_broadcast([P, n, NB, WIN]), ALU.mult).then_inc(win_ready, 1)

                window(0, 0)
                ok = dve.value_load(flag[0:1, 0:1], min_val=0, max_val=1)
                with dve.If(ok == 1):
                    at = [dve.alloc_register(f"at{s}") for s in range(SLOTS)]

                    def positions(t, n=SLOTS):
                        dve.load(at[0:n], pos_row[0:1, bass.ds(t, n)])
                        return [dve.snap(r, min_val=0, max_val=RING - 1) for r in at[0:n]]

                    def add_part(t, s, where):
                        dve.wait_ge(part_ready, t + 1)
                        dve.wait_ge(part_added, t + 1)
                        ring = sums[:, :, bass.ds(where[s % SLOTS], WIN)]
                        v.tensor_tensor(ring, ring, part[:, s % PARTS, :].rearrange("p (c n) -> p c n", n=WIN),
                                        ALU.add).then_inc(part_added, 1)

                    def fold(k, done):
                        if not isinstance(k, int) or k >= 1:
                            dve.wait_ge(cleaned, UNITS * k)
                        dve.wait_ge(part_added, done + 1)
                        v.tensor_tensor(sums[:, :, 0:WIN], sums[:, :, 0:WIN], sums[:, :, RING:RING + WIN],
                                        ALU.add).then_inc(folded, 1)
                        dve.wait_ge(folded, 2 * k + 1)
                        v.memset(sums[:, :, RING:RING + WIN], 0.0).then_inc(folded, 1)

                    def split(k, u):
                        dve.wait_ge(unit_copied, k * UNITS + u + 1)
                        for i in range(2):
                            n = slice(i * HALF, (i + 1) * HALF)
                            r = v.tensor_tensor(unit_l[:, u % 2, :, n],
                                                sums[:, u * UNIT:(u + 1) * UNIT, bass.ds((k * BLK + i * HALF) % RING, HALF)],
                                                unit_h[:, u % 2, :, n].bitcast(F32), ALU.subtract)
                        r.then_inc(unit_split, 1)

                    def evacuate(k, n):
                        dve.wait_ge(block_done, k + 2)
                        dve.wait_ge(x_in, 16 * k + 16)
                        v.tensor_tensor(y[0:n, :], out_ps[0:n, :], y[0:n, :], ALU.add).then_inc(evacuated, 1)

                    def norm(k, n, i):
                        if i == 0:
                            dve.wait_ge(evacuated, k + 2)
                            v.tensor_tensor(y[0:n, :], y[0:n, :], bias_all[0:n, :], ALU.add).then_inc(norm_v, 1)
                        if i == 1:
                            dve.wait_ge(norm_v, 5 * k + 1)
                            v.bn_stats(stats[0:n, :], y[0:n, :]).then_inc(norm_v, 1)
                            dve.wait_ge(norm_v, 5 * k + 2)
                            dve.sem_inc(dve_turns, 1)
                            v.bn_aggr(mv[0:n, :], stats[0:n, :]).then_inc(norm_v, 1)
                        if i == 2:
                            dve.wait_ge(norm_a, 2 * k + 1)
                            v.reciprocal(sd[0:n, 1:2], sd[0:n, 0:1]).then_inc(norm_v, 1)
                            dve.wait_ge(norm_v, 5 * k + 4)
                            v.tensor_scalar(sd[0:n, 2:3], mv[0:n, 0:1], sd[0:n, 1:2], -1.0, ALU.mult, ALU.mult).then_inc(norm_v, 1)

                    def bases_low(i):
                        dve.wait_ge(high_ready, i + 1)
                        v.tensor_tensor(bases_l[:, i, :], raw[:, i, :], bases_h[:, i, :].bitcast(F32), ALU.subtract).then_inc(low_ready, 1)

                    for t in range(HEAD):
                        if t % SLOTS == 0:
                            where = positions(t)
                        add_part(t, t, where)
                        if t % SLOTS == 1:
                            g = t // SLOTS + 1
                            if g % 2 == 0:
                                dve.wait_ge(coef_ready, g * SLOTS // BT + 1)
                            window(g, g % 2)
                        i = t // 2 + PRE
                        if t % 2 == 0 and i < NSB:
                            coefs(i)
                        if t % 2 == 1 and i + 1 < NSB:
                            hot(i + 1)
                        for j in low_at(t):
                            bases_low(j)
                    dve.wait_ge(coef_ready, NSB)

                    def step(k, p, where, last=T):
                        t = k * TPB + (HEAD + p)
                        if not isinstance(t, int) or t < last:
                            g = k * GPB + (HEAD + p) // SLOTS
                            if p % SLOTS == 0:
                                where = positions(t, min(SLOTS, last - t) if isinstance(t, int) else SLOTS)
                            add_part(t, p, where)
                            if p % SLOTS == 1:
                                window(g + 1, ((HEAD + p) // SLOTS + 1) % 2,
                                       min(SLOTS, last - (g + 1) * SLOTS) if isinstance(g, int) else SLOTS)
                        if p % UNIT == 1 and p // UNIT < LOWS:
                            split(k, p // UNIT)
                        if isinstance(k, int) and k == 0:
                            for j in low_at(t):
                                bases_low(j)
                        return where

                    def opening(k, where):
                        for p in range(SLOTS):
                            where = step(k, p, where)
                            if not (isinstance(k, int) and k == 0) and p < 3:
                                norm(k - 1, BLK, p)
                        return where

                    dve.wait_ge(bias_in, 16)
                    fold(0, HEAD)
                    where = opening(0, where)
                    for p in range(SLOTS, TPB):
                        where = step(0, p, where)
                    with dve.Fori(0, NBLK - 3) as k:
                        fold(k + 1, k * TPB + (HEAD + TPB))
                        evacuate(k, BLK)
                        where = opening(k + 1, where)
                        for p in range(SLOTS, TPB):
                            where = step(k + 1, p, where)
                    k = NBLK - 3
                    fold(k + 1, k * TPB + (HEAD + TPB))
                    evacuate(k, BLK)
                    where = opening(k + 1, where)
                    for p in range(SLOTS, TPB):
                        where = step(NBLK - 2, p, where)
                    fold(NBLK - 1, T)
                    evacuate(NBLK - 2, BLK)
                    for u in range(LOWS):
                        split(NBLK - 1, u)
                        if u < 3:
                            norm(NBLK - 2, BLK, u)
                    n = N - (NBLK - 1) * BLK
                    evacuate(NBLK - 1, n)
                    for i in range(3):
                        norm(NBLK - 1, n, i)
                with dve.Else():
                    dve.wait_ge(transposed, 5)
                    v.tensor_copy(dstc[:, :], banks[:, 3, 0:TG]).then_inc(tables, 1)
                    for i in range(PRE, NSB):
                        if i + 1 < NSB:
                            hot(i + 1)
                        coefs(i)
                    dve.wait_ge(coef_ready, NSB)
                    dve.wait_ge(tables, 4)
                    dve.wait_ge(bias_in, 16)
                    gr = slice(0, GEN)
                    dve.sem_inc(g_sum, 1)
                    with dve.Fori(0, N // GEN) as w:
                        with dve.Fori(0, T) as t:
                            dve.wait_ge(g_step, w * T + t + 1)
                            v.scalar_tensor_tensor(
                                gwin, node_iota[:, :].unsqueeze(1).to_broadcast([P, NB, GEN]),
                                dstc[:, bass.ds(t, 1)],
                                coef[:, bass.ds(t, 1), :].rearrange("p o b -> p (o b)").unsqueeze(2).to_broadcast([P, NB, GEN]),
                                ALU.is_equal, ALU.mult).then_inc(g_win, 1)
                        dve.wait_ge(g_mm, w * T + T)
                        for c in range(IC):
                            v.tensor_copy(gsum[:, c * NB:(c + 1) * NB, :], banks[:, c, 0:NB * GEN].rearrange("p (b n) -> p b n", b=NB))
                        v.tensor_scalar(dstc[:, :], dstc[:, :], float(-GEN), None, ALU.add).then_inc(g_sum, 1)
                        dve.wait_ge(g_sum, w + 2)
                        dve.sem_inc(g_out, 1)
                        dve.wait_ge(g_done, w + 1)
                        dve.wait_ge(g_x, 16 * w + 16)
                        v.tensor_tensor(y[gr, :], out_ps[gr, :], y[gr, :], ALU.add).then_inc(g_v, 1)
                        dve.wait_ge(g_v, 6 * w + 1)
                        v.tensor_tensor(y[gr, :], y[gr, :], bias_all[gr, :], ALU.add).then_inc(g_v, 1)
                        dve.wait_ge(g_v, 6 * w + 2)
                        v.bn_stats(stats[gr, :], y[gr, :]).then_inc(g_v, 1)
                        dve.wait_ge(g_v, 6 * w + 3)
                        dve.sem_inc(dve_turns, 1)
                        v.bn_aggr(mv[gr, :], stats[gr, :]).then_inc(g_v, 1)
                        dve.wait_ge(g_a, 2 * w + 1)
                        v.reciprocal(sd[gr, 1:2], sd[gr, 0:1]).then_inc(g_v, 1)
                        dve.wait_ge(g_v, 6 * w + 5)
                        v.tensor_scalar(sd[gr, 2:3], mv[gr, 0:1], sd[gr, 1:2], -1.0, ALU.mult, ALU.mult).then_inc(g_v, 1)
                        dve.wait_ge(g_w, 16 * w + 16)

            @block.scalar
            def _(act):
                a = nc.scalar
                act.wait_ge(consts, 1)
                a.activation(pick.rearrange("p (t r) -> p t r", r=R), ident[:, :].unsqueeze(2).to_broadcast([P, P, R]),
                             ACT.Copy).then_inc(picked, 1)
                act.wait_ge(swept, 2)
                a.activation(sums[:, POOL_PLANES:PL, :], zero[:, 0:1].unsqueeze(2).to_broadcast([P, PL - POOL_PLANES, RING + WIN]),
                             ACT.Copy).then_inc(swept, 1)

                def types(i):
                    nq = min(SB, QN - i * SB)
                    act.wait_ge(type_done, i + 1)
                    if i >= 2:
                        act.wait_ge(hot_ready, i)
                    a.activation(et_all[:, i % 2, 0:nq, :], type_ps[:, 0:nq * P].rearrange("p (q e) -> p q e", e=P), ACT.Copy).then_inc(type_copied, 1)
                for i in range(PRE + 1):
                    types(i)

                def load_bias():
                    act.wait_ge(coef_done, NSB)
                    act.dma_start(bias_all[:, :], h_bias.partition_broadcast(P)).then_inc(bias_in, 16)
                act.wait_ge(flag_ready, 1)
                ok = act.value_load(flag[0:1, 0:1], min_val=0, max_val=1)
                with act.If(ok == 1):
                    act.sem_inc(unit_free, 1)
                    act.sem_inc(block_done, 1)
                    act.sem_inc(evacuated, 1)
                    act.sem_inc(part_added, 1)
                    act.sem_inc(out_written, 1)
                    def high(i):
                        if i % RAWS == 0:
                            act.wait_ge(raw_in[i // RAWS], 16)
                        a.activation(bases_h[:, i, :], raw[:, i, :], ACT.Copy).then_inc(high_ready, 1)
                    act.wait_ge(transposed, 4)
                    act.wait_ge(idx_out, 16)
                    for s in range(SLOTS):
                        act.wait_ge(row_in[s], 16)
                    for t in range(HEAD):
                        if t % 2 == 0 and t // 2 + PRE + 1 < NSB:
                            types(t // 2 + PRE + 1)
                        for i in high_at(t):
                            high(i)
                    load_bias()

                    def unit(k, u):
                        if u == 0:
                            act.wait_ge(folded, 2 * k + 2)
                            act.wait_ge(unit_free, k * (UNITS - 1) + 1)
                        elif u == 1:
                            act.wait_ge(block_done, k + 1)
                        else:
                            act.wait_ge(unit_free, k * (UNITS - 1) + u)
                        act.sem_inc(act_turns, 1)
                        to = unit_h if u < LOWS else unit_f
                        b = u % 2 if u < LOWS else u - LOWS
                        planes = [sums[:, u * UNIT:(u + 1) * UNIT, bass.ds((k * BLK + i * HALF) % RING, HALF)] for i in range(2)]
                        for i in range(2):
                            r = a.activation(to[:, b, :, i * HALF:(i + 1) * HALF], planes[i], ACT.Copy)
                        r.then_inc(unit_copied, 1)
                        if u < LOWS:
                            act.wait_ge(unit_split, k * LOWS + u + 1)
                        else:
                            act.wait_ge(unit_copied, k * UNITS + u + 1)
                        act.sem_inc(act_turns, 1)
                        for i in range(2):
                            r = a.activation(planes[i], zero[:, 0:1].unsqueeze(2).to_broadcast([P, UNIT, HALF]), ACT.Copy)
                        r.then_inc(cleaned, 1)

                    def load_x(k, rows_x, n):
                        act.wait_ge(out_written, 16 * k + 1)
                        act.dma_start(y[0:n, :], rows_x).then_inc(x_in, 16)

                    def deviation(k, n):
                        act.wait_ge(norm_v, 5 * k + 3)
                        a.activation(sd[0:n, 0:1], mv[0:n, 1:2], ACT.Sqrt, bias=eps[0:n, 0:1]).then_inc(norm_a, 1)

                    def finish(k, n, out_k):
                        act.wait_ge(norm_v, 5 * k + 5)
                        a.activation(y[0:n, :], y[0:n, :], ACT.Identity, bias=sd[0:n, 2:3],
                                     scale=sd[0:n, 1:2]).then_inc(norm_a, 1)
                        act.wait_ge(norm_a, 2 * k + 2)
                        act.dma_start(out_k, y[0:n, :]).then_inc(out_written, 16)

                    unit(0, 0)
                    unit(0, 1)
                    with act.Fori(0, NBLK - 2) as k:
                        for u in range(2, UNITS):
                            if u == UNITS - 2:
                                load_x(k, x[bass.ds(k * BLK, BLK), :], BLK)
                            unit(k, u)
                        unit(k + 1, 0)
                        deviation(k, BLK)
                        unit(k + 1, 1)
                        finish(k, BLK, out[bass.ds(k * BLK, BLK), :])
                    k = NBLK - 2
                    n = N - (NBLK - 1) * BLK
                    for u in range(2, UNITS):
                        if u == UNITS - 2:
                            load_x(k, x[k * BLK:k * BLK + BLK, :], BLK)
                        unit(k, u)
                    unit(k + 1, 0)
                    unit(k + 1, 1)
                    deviation(k, BLK)
                    unit(k + 1, 2)
                    finish(k, BLK, out[k * BLK:k * BLK + BLK, :])
                    for u in range(3, UNITS):
                        if u == UNITS - 2:
                            load_x(k + 1, x[k * BLK + BLK:N, :], n)
                        unit(k + 1, u)
                    deviation(k + 1, n)
                    finish(k + 1, n, out[k * BLK + BLK:N, :])
                    act.wait_ge(out_written, 16 * NBLK + 1)
                with act.Else():
                    for i in range(PRE + 1, NSB):
                        types(i)
                    load_bias()
                    for i in range(0, PL - SPLIT, RAWS):
                        load_whole(act, i, RAWS)
                    gr = slice(0, GEN)
                    for s in range(SLOTS):
                        act.wait_ge(row_in[s], 16)
                    for p in range(4):
                        act.sem_inc(g_used, 1)
                    with act.Fori(0, N // GEN) as w:
                        act.dma_start(y[gr, :], x[bass.ds(w * GEN, GEN), :]).then_inc(g_x, 16)

                        def step(i, t, b):
                            a.copy(gidx[:, b:b + 1], idx[:, bass.ds(t, 1)]).then_inc(g_idx, 1)
                            act.sem_inc(g_step, 1)
                            act.wait_ge(g_mm, i + 1)
                        with act.Fori(0, T // 2) as h:
                            step(w * T + 2 * h, 2 * h, 0)
                            step(w * T + 2 * h + 1, 2 * h + 1, 1)
                        step(w * T + T - 1, T - 1, 0)
                        act.wait_ge(g_v, 6 * w + 4)
                        a.activation(sd[gr, 0:1], mv[gr, 1:2], ACT.Sqrt, bias=eps[gr, 0:1]).then_inc(g_a, 1)
                        act.wait_ge(g_v, 6 * w + 6)
                        a.activation(y[gr, :], y[gr, :], ACT.Identity, bias=sd[gr, 2:3], scale=sd[gr, 1:2]).then_inc(g_a, 1)
                        act.wait_ge(g_a, 2 * w + 2)
                        act.dma_start(out[bass.ds(w * GEN, GEN), :], y[gr, :]).then_inc(g_w, 16)
                        act.wait_ge(g_w, 16 * w + 16)


_INS = ["x", "src", "dst", "edge_type_32", "edge_weight1", "L0_gnn_bases", "L0_gnn_w_comp", "L0_gnn_h_bias"]


def kernel(**inputs):
    import numpy as np
    import concourse.bacc as bacc
    from concourse import mybir
    from concourse.bass_utils import run_bass_kernel_spmd

    nc = bacc.Bacc("TRN2", target_bir_lowering=False, num_devices=1)
    arrays, args = {}, []
    for name in _INS:
        a = np.ascontiguousarray(inputs[name])
        arrays[f"in_{name}"] = a
        args.append(nc.dram_tensor(f"in_{name}", a.shape, mybir.dt.from_np(a.dtype), kind="ExternalInput").ap())
    args.append(nc.dram_tensor("out", inputs["x"].shape, mybir.dt.float32, kind="ExternalOutput").ap())
    rgcn_resnorm(nc, *args)
    r = run_bass_kernel_spmd(nc, [arrays], core_ids=[0])
    return r.results[0]["out"]
```
